# Optimizing a Trainium2 kernel written in Bass

```python
import numpy as np
import jax
import jax.numpy as jnp

def _softmax(x, axis=-1):
    return jax.nn.softmax(x, axis=axis)

def _gelu(x):
    return jax.nn.gelu(x, approximate=True)

def _silu(x):
    return jax.nn.silu(x)

def _sigmoid(x):
    return jax.nn.sigmoid(x)

def _layernorm(x, axis=-1, eps=1e-05):
    m = jnp.mean(x, axis=axis, keepdims=True)
    v = jnp.var(x, axis=axis, keepdims=True)
    return (x - m) / jnp.sqrt(v + eps)

def _scatter_add(tgt, idx, src, axis=0):
    return tgt.at[idx].add(src)

def _segment_sum(src, seg, n):
    return jax.ops.segment_sum(src, seg, n)
kernel_name = 'mk_hybrid_d1_jaxref_r8_3eaab5'

def setup_inputs(seed: int=0):
    np.random.seed(seed)
    _w = jnp.asarray

    def _L0_attn_a_setup():
        import jax, jax.numpy as jnp
        import numpy as np
        D_MODEL = 128
        N_HEAD = 16
        HEAD_DIM = D_MODEL // N_HEAD
        key = jax.random.key(seed)
        k1, k2, k3 = jax.random.split(key, 3)
        B, T, C = (4, 256, D_MODEL)
        x = jax.random.normal(k1, (B, T, C), dtype=jnp.float32)
        w_qkv = jax.random.normal(k2, (3 * C, C), dtype=jnp.float32) * (1.0 / np.sqrt(C))
        w_out = jax.random.normal(k3, (C, C), dtype=jnp.float32) * (1.0 / np.sqrt(C))
        return {'x': x, 'w_qkv': w_qkv, 'w_out': w_out}
    _L0_attn_a_in = _L0_attn_a_setup()

    def _L0_attn_b_setup():
        import jax, jax.numpy as jnp
        import numpy as np
        D_MODEL = 128
        NHEAD = 16
        HEAD_DIM = D_MODEL // NHEAD
        SCALE = HEAD_DIM ** (-0.5)
        EPS_LN = 1e-05
        key = jax.random.key(seed)
        ks = jax.random.split(key, 7)
        B, T, D = (2, 256, D_MODEL)
        x = jax.random.normal(ks[0], (B, T, D), dtype=jnp.float32)
        ln_gamma = jnp.ones((D,), dtype=jnp.float32)
        ln_beta = jnp.zeros((D,), dtype=jnp.float32)
        s = 1.0 / np.sqrt(D)
        W_qkv = jax.random.uniform(ks[1], (D, 3 * D), minval=-s, maxval=s, dtype=jnp.float32)
        b_qkv = jax.random.uniform(ks[2], (3 * D,), minval=-s, maxval=s, dtype=jnp.float32)
        W_proj = jax.random.uniform(ks[3], (D, D), minval=-s, maxval=s, dtype=jnp.float32)
        b_proj = jax.random.uniform(ks[4], (D,), minval=-s, maxval=s, dtype=jnp.float32)
        return {'x': x, 'ln_gamma': ln_gamma, 'ln_beta': ln_beta, 'W_qkv': W_qkv, 'b_qkv': b_qkv, 'W_proj': W_proj, 'b_proj': b_proj}
    _L0_attn_b_in = _L0_attn_b_setup()

    def _L0_ffn_setup():
        import jax, jax.numpy as jnp
        import numpy as np
        B, S, DIM = (4, 512, 128)
        BASE_COUPLING = 0.1
        NUM_CYCLES = 3

        def _gelu(x):
            return jax.nn.gelu(x, approximate=False)

        def _coupling_net(h, w1, b1, w2, b2, w3, b3, w4, b4):
            h = _gelu(h @ w1 + b1)
            h = _gelu(h @ w2 + b2)
            h = _gelu(h @ w3 + b3)
            return jax.nn.sigmoid(h @ w4 + b4)

        def _global_net(h, w1, b1, w2, b2, w3, b3):
            h = _gelu(h @ w1 + b1)
            h = _gelu(h @ w2 + b2)
            return jax.nn.sigmoid(h @ w3 + b3)

        def _twist(x):
            o_r, o_i, p_r, p_i = jnp.split(x, 4, axis=-1)
            return jnp.concatenate([p_r, -p_i, -o_r, o_i], axis=-1)
        key = jax.random.key(seed)
        ks = jax.random.split(key, 9)
        d = DIM

        def w(k, fan_in, fan_out):
            return jax.random.normal(k, (fan_in, fan_out), dtype=jnp.float32) / np.sqrt(fan_in).astype(np.float32)
        inp = {'x': jax.random.normal(ks[0], (B, S, d), dtype=jnp.float32)}
        cn_dims = [(d, d), (d, d // 2), (d // 2, d // 4), (d // 4, 1)]
        for i, (a, b) in enumerate(cn_dims):
            inp[f'cn_w{i + 1}'] = w(ks[1 + i], a, b)
            inp[f'cn_b{i + 1}'] = jnp.zeros((b,), dtype=jnp.float32)
        gc_dims = [(d, d // 2), (d // 2, d // 4), (d // 4, 1)]
        for i, (a, b) in enumerate(gc_dims):
            inp[f'gc_w{i + 1}'] = w(ks[5 + i], a, b)
            inp[f'gc_b{i + 1}'] = jnp.zeros((b,), dtype=jnp.float32)
        inp['adaptive_range'] = jnp.full((1,), 0.2, dtype=jnp.float32)
        return inp
    _L0_ffn_in = _L0_ffn_setup()
    _d = {'L0_attn_a_x': _L0_attn_a_in['x'], 'L0_attn_a_w_qkv': _L0_attn_a_in['w_qkv'], 'L0_attn_a_w_out': _L0_attn_a_in['w_out'], 'L0_attn_b_ln_gamma': _L0_attn_b_in['ln_gamma'], 'L0_attn_b_ln_beta': _L0_attn_b_in['ln_beta'], 'L0_attn_b_W_qkv': _L0_attn_b_in['W_qkv'], 'L0_attn_b_b_qkv': _L0_attn_b_in['b_qkv'], 'L0_attn_b_W_proj': _L0_attn_b_in['W_proj'], 'L0_attn_b_b_proj': _L0_attn_b_in['b_proj'], 'L0_ffn_cn_w1': _L0_ffn_in['cn_w1'], 'L0_ffn_cn_b1': _L0_ffn_in['cn_b1'], 'L0_ffn_cn_w2': _L0_ffn_in['cn_w2'], 'L0_ffn_cn_b2': _L0_ffn_in['cn_b2'], 'L0_ffn_cn_w3': _L0_ffn_in['cn_w3'], 'L0_ffn_cn_b3': _L0_ffn_in['cn_b3'], 'L0_ffn_cn_w4': _L0_ffn_in['cn_w4'], 'L0_ffn_cn_b4': _L0_ffn_in['cn_b4'], 'L0_ffn_gc_w1': _L0_ffn_in['gc_w1'], 'L0_ffn_gc_b1': _L0_ffn_in['gc_b1'], 'L0_ffn_gc_w2': _L0_ffn_in['gc_w2'], 'L0_ffn_gc_b2': _L0_ffn_in['gc_b2'], 'L0_ffn_gc_w3': _L0_ffn_in['gc_w3'], 'L0_ffn_gc_b3': _L0_ffn_in['gc_b3'], 'L0_ffn_adaptive_range': _L0_ffn_in['adaptive_range']}
    _x0 = _d['L0_attn_a_x']
    _d['L0_attn_a_x'] = jax.random.normal(jax.random.fold_in(jax.random.key(seed), 1), (16, 256, 128), dtype=_x0.dtype)
    del _x0
    return _d

def reference(L0_attn_a_x, L0_attn_a_w_qkv, L0_attn_a_w_out, L0_attn_b_ln_gamma, L0_attn_b_ln_beta, L0_attn_b_W_qkv, L0_attn_b_b_qkv, L0_attn_b_W_proj, L0_attn_b_b_proj, L0_ffn_cn_w1, L0_ffn_cn_b1, L0_ffn_cn_w2, L0_ffn_cn_b2, L0_ffn_cn_w3, L0_ffn_cn_b3, L0_ffn_cn_w4, L0_ffn_cn_b4, L0_ffn_gc_w1, L0_ffn_gc_b1, L0_ffn_gc_w2, L0_ffn_gc_b2, L0_ffn_gc_w3, L0_ffn_gc_b3, L0_ffn_adaptive_range):

    def _L0_attn_a_ref(x, w_qkv, w_out):
        import jax, jax.numpy as jnp
        import numpy as np
        D_MODEL = 128
        N_HEAD = 16
        HEAD_DIM = D_MODEL // N_HEAD
        B, T, C = x.shape
        H, Dh = (N_HEAD, HEAD_DIM)
        qkv = jnp.einsum('btc,fc->btf', x, w_qkv)
        q, k, v = jnp.split(qkv, 3, axis=-1)
        q = q.reshape(B, T, H, Dh).transpose(0, 2, 1, 3)
        k = k.reshape(B, T, H, Dh).transpose(0, 2, 1, 3)
        v = v.reshape(B, T, H, Dh).transpose(0, 2, 1, 3)
        scale = 1.0 / np.sqrt(Dh).astype(np.float32)
        att = jnp.einsum('bhqd,bhkd->bhqk', q, k) * scale
        causal = jnp.tril(jnp.ones((T, T), dtype=bool))
        att = jnp.where(causal[None, None], att, -jnp.inf)
        att = jax.nn.softmax(att, axis=-1)
        y = jnp.einsum('bhqk,bhkd->bhqd', att, v)
        y = y.transpose(0, 2, 1, 3).reshape(B, T, C)
        return jnp.einsum('btc,fc->btf', y, w_out)

    def _L0_attn_b_ref(x, ln_gamma, ln_beta, W_qkv, b_qkv, W_proj, b_proj):
        import jax, jax.numpy as jnp
        import numpy as np
        D_MODEL = 128
        NHEAD = 16
        HEAD_DIM = D_MODEL // NHEAD
        SCALE = HEAD_DIM ** (-0.5)
        EPS_LN = 1e-05
        B, T, D = x.shape
        h, dh = (NHEAD, HEAD_DIM)
        mu = jnp.mean(x, axis=-1, keepdims=True)
        var = jnp.mean(jnp.square(x - mu), axis=-1, keepdims=True)
        x_n = (x - mu) * jax.lax.rsqrt(var + EPS_LN) * ln_gamma + ln_beta
        qkv = x_n @ W_qkv + b_qkv
        q, k, v = jnp.split(qkv, 3, axis=-1)
        q = q.reshape(B, T, h, dh).transpose(0, 2, 1, 3)
        k = k.reshape(B, T, h, dh).transpose(0, 2, 1, 3)
        v = v.reshape(B, T, h, dh).transpose(0, 2, 1, 3)
        scores = jnp.einsum('bhqd,bhkd->bhqk', q, k) * SCALE
        scores = scores - jnp.max(scores, axis=-1, keepdims=True)
        attn = jnp.exp(scores)
        attn = attn / jnp.maximum(jnp.sum(attn, axis=-1, keepdims=True), 1e-12)
        ctx = jnp.einsum('bhqk,bhkd->bhqd', attn, v)
        ctx = ctx.transpose(0, 2, 1, 3).reshape(B, T, D)
        return ctx @ W_proj + b_proj

    def _L0_ffn_ref(x, cn_w1, cn_b1, cn_w2, cn_b2, cn_w3, cn_b3, cn_w4, cn_b4, gc_w1, gc_b1, gc_w2, gc_b2, gc_w3, gc_b3, adaptive_range):
        import jax, jax.numpy as jnp
        import numpy as np
        B, S, DIM = (4, 512, 128)
        BASE_COUPLING = 0.1
        NUM_CYCLES = 3

        def _gelu(x):
            return jax.nn.gelu(x, approximate=False)

        def _coupling_net(h, w1, b1, w2, b2, w3, b3, w4, b4):
            h = _gelu(h @ w1 + b1)
            h = _gelu(h @ w2 + b2)
            h = _gelu(h @ w3 + b3)
            return jax.nn.sigmoid(h @ w4 + b4)

        def _global_net(h, w1, b1, w2, b2, w3, b3):
            h = _gelu(h @ w1 + b1)
            h = _gelu(h @ w2 + b2)
            return jax.nn.sigmoid(h @ w3 + b3)

        def _twist(x):
            o_r, o_i, p_r, p_i = jnp.split(x, 4, axis=-1)
            return jnp.concatenate([p_r, -p_i, -o_r, o_i], axis=-1)
        global_context = x.mean(axis=1, keepdims=True)
        gf = _global_net(global_context, gc_w1, gc_b1, gc_w2, gc_b2, gc_w3, gc_b3)
        out = x
        for _ in range(NUM_CYCLES):
            tf = _coupling_net(out, cn_w1, cn_b1, cn_w2, cn_b2, cn_w3, cn_b3, cn_w4, cn_b4)
            combined = 0.7 * gf + 0.3 * tf
            coupling = BASE_COUPLING + adaptive_range * (combined - 0.5) * 2.0
            out = out + coupling * _twist(out)
        return out
    x = L0_attn_a_x
    x = x + _L0_attn_a_ref(_layernorm(x, axis=-1), L0_attn_a_w_qkv, L0_attn_a_w_out)
    x = x + _L0_ffn_ref(_layernorm(x, axis=-1), L0_ffn_cn_w1, L0_ffn_cn_b1, L0_ffn_cn_w2, L0_ffn_cn_b2, L0_ffn_cn_w3, L0_ffn_cn_b3, L0_ffn_cn_w4, L0_ffn_cn_b4, L0_ffn_gc_w1, L0_ffn_gc_b1, L0_ffn_gc_w2, L0_ffn_gc_b2, L0_ffn_gc_w3, L0_ffn_gc_b3, L0_ffn_adaptive_range)
    x = x + _L0_attn_b_ref(_layernorm(x, axis=-1), L0_attn_b_ln_gamma, L0_attn_b_ln_beta, L0_attn_b_W_qkv, L0_attn_b_b_qkv, L0_attn_b_W_proj, L0_attn_b_b_proj)
    x = x + _L0_ffn_ref(_layernorm(x, axis=-1), L0_ffn_cn_w1, L0_ffn_cn_b1, L0_ffn_cn_w2, L0_ffn_cn_b2, L0_ffn_cn_w3, L0_ffn_cn_b3, L0_ffn_cn_w4, L0_ffn_cn_b4, L0_ffn_gc_w1, L0_ffn_gc_b1, L0_ffn_gc_w2, L0_ffn_gc_b2, L0_ffn_gc_w3, L0_ffn_gc_b3, L0_ffn_adaptive_range)
    return x

_drawn_inputs = setup_inputs


def setup_inputs(seed=0):
    import zlib

    import numpy as np

    out = dict(_drawn_inputs(seed))
    spreads = {'L0_attn_b_ln_gamma': (1.0, 0.6),
     'L0_attn_b_ln_beta': (0.0, 0.532),
     'L0_ffn_cn_b1': (0.0, 0.8),
     'L0_ffn_cn_b2': (0.0, 2.0),
     'L0_ffn_cn_b3': (0.0, 2.0),
     'L0_ffn_gc_b1': (0.0, 0.8),
     'L0_ffn_gc_b2': (0.0, 0.8)}
    factors = {'L0_attn_b_b_qkv': 3.677,
     'L0_ffn_cn_w1': 4.996,
     'L0_ffn_cn_w2': 4.695,
     'L0_ffn_cn_w3': 4.037,
     'L0_ffn_gc_w1': 8.0,
     'L0_ffn_gc_w2': 6.465,
     'L0_ffn_gc_w3': 8.0}
    for name, (base, spread) in spreads.items():
        noise = np.random.default_rng([zlib.crc32(name.encode()), seed]).standard_normal(out[name].shape)
        drawn = base * np.exp(spread * noise) if base else spread * noise
        out[name] = jnp.asarray(drawn.astype(out[name].dtype))
    for name, factor in factors.items():
        out[name] = (out[name] * factor).astype(out[name].dtype)
    return out
```

```python
from contextlib import ExitStack

import numpy as np
import concourse.bass as bass
from concourse import mybir
from concourse.alu_op_type import AluOpType as ALU

ACT = mybir.ActivationFunctionType
F32 = mybir.dt.float32
F32R = mybir.dt.float32r
AX = mybir.AxisListType.X

NB, T, D = 16, 256, 128
P = 128
NT = NB * T // P
H, DH = 16, 8
G, HG = 4, 4
GW = HG * DH
SL = 3 * GW
VB = 48
EPS = 1e-5
NEG = -1e30
CH = 512
NCH = NB * T // CH
CYCLES = 3


def wait(eng, sem, value):
    if isinstance(value, int) and value <= 0:
        return
    eng.wait_ge(sem, value)


def over_batches(eng, body):
    for b in (0, 1):
        body(b, b % 2, b > 0, True, True)
    with eng.Fori(1, NB // 2 - 1) as it:
        body(2 * it, 0, True, True, True)
        body(2 * it + 1, 1, True, True, True)
    for b in (NB - 2, NB - 1):
        body(b, b % 2, True, b < NB - 1, False)


def build(nc, x, w_qkv, w_out, ln_gamma, ln_beta, W_qkv, b_qkv, W_proj, b_proj,
          cn_w1, cn_b1, cn_w2, cn_b2, cn_w3, cn_b3, cn_w4, cn_b4,
          gc_w1, gc_b1, gc_w2, gc_b2, gc_w3, gc_b3, adaptive_range, out):
    with ExitStack() as ctx:
        def sb(name, shape, dt=F32):
            return ctx.enter_context(nc.sbuf_tensor(name, shape, dt))

        S = {}
        S["X"] = sb("X", [P, NT, D])
        S["ident"] = sb("ident", [P, P])
        S["minus_half"] = sb("minus_half", [P, 4])
        S["ident_r"] = sb("ident_r", [P, P], F32R)
        S["causal_qk"] = sb("causal_qk", [P, P], F32R)
        S["causal_kq"] = sb("causal_kq", [P, P], F32R)
        S["head_rows"] = sb("head_rows", [P, HG])
        S["max_row"] = sb("max_row", [P, HG])
        for ph in "ab":
            S["wqk" + ph] = sb("wqk" + ph, [P, 2, G, SL])
            S["wv" + ph] = sb("wv" + ph, [P, D])
            S["wo" + ph] = sb("wo" + ph, [P, D])
        S["bqk"] = sb("bqk", [SL, 2, G])
        S["bv"] = sb("bv", [P, D])
        S["bproj"] = sb("bproj", [P, D])
        S["gamma"] = sb("gamma", [P, 1])
        S["beta"] = sb("beta", [P, 1])
        S["w1"] = sb("w1", [P, D])
        S["w2"] = sb("w2", [P, D // 2])
        S["w3"] = sb("w3", [P, D // 2])
        S["w4"] = sb("w4", [P, P])
        S["w4c"] = sb("w4c", [P, 1])
        S["cb1"] = sb("cb1", [P, 1])
        S["cb2"] = sb("cb2", [P, 1])
        S["cb3"] = sb("cb3", [P, 1])
        S["cb4"] = sb("cb4", [P, 1])
        S["g1"] = sb("g1", [P, D // 2])
        S["g2"] = sb("g2", [D // 2, D // 4])
        S["g3"] = sb("g3", [D // 4, P])
        S["g3c"] = sb("g3c", [D // 4, 1])
        S["gb1"] = sb("gb1", [D // 2, 1])
        S["gb2"] = sb("gb2", [D // 4, 1])
        S["gb3"] = sb("gb3", [P, 1])
        S["ar"] = sb("ar", [P, 1])
        S["ar3"] = sb("ar3", [P, 1])
        S["ar7"] = sb("ar7", [P, 1])
        S["twist"] = sb("twist", [P, P])
        S["pick"] = sb("pick", [P, 4, P], F32R)

        setup(nc, S, x, w_qkv, w_out, ln_gamma, ln_beta, W_qkv, b_qkv, W_proj, b_proj,
              cn_w1, cn_b1, cn_w2, cn_b2, cn_w3, cn_b3, cn_w4, cn_b4,
              gc_w1, gc_b1, gc_w2, gc_b2, gc_w3, gc_b3, adaptive_range)
        attention(nc, S, "a")
        feed_forward(nc, S, "f", None)
        attention(nc, S, "b")
        feed_forward(nc, S, "s", out)


def setup(nc, S, x, w_qkv, w_out, ln_gamma, ln_beta, W_qkv, b_qkv, W_proj, b_proj,
          cn_w1, cn_b1, cn_w2, cn_b2, cn_w3, cn_b3, cn_w4, cn_b4,
          gc_w1, gc_b1, gc_w2, gc_b2, gc_w3, gc_b3, adaptive_range):
    with ExitStack() as ctx:
        wa = ctx.enter_context(nc.sbuf_tensor("set_wa", [P, 3, D], F32))
        woa = ctx.enter_context(nc.sbuf_tensor("set_woa", [P, D], F32))
        woap = ctx.enter_context(nc.sbuf_tensor("woap", [P, D], F32))
        wb = ctx.enter_context(nc.sbuf_tensor("set_wb", [P, 3 * D], F32))
        band = ctx.enter_context(nc.sbuf_tensor("band", [P, HG, 4], F32))
        mask = ctx.enter_context(nc.sbuf_tensor("mask", [P, 2, P], F32))
        pickf = ctx.enter_context(nc.sbuf_tensor("pickf", [P, 4, P], F32))
        blocks = ctx.enter_context(nc.sbuf_tensor("blocks", [P, 4, GW], F32))
        ps = ctx.enter_context(nc.psum_tensor("ps_setup", [P, 2, 512], F32))

        def sem(name):
            return ctx.enter_context(nc.semaphore("set_" + name))
        x_in, w_in = sem("x_in"), sem("w_in")
        zeroed, shaped, made = sem("zeroed"), sem("shaped"), sem("made")
        permuted, turned = sem("permuted"), sem("turned")
        ctx.enter_context(nc.allow_non_contiguous_dma(reason="a few hundred bias values, once"))
        block = ctx.enter_context(nc.Block())
        X = S["X"]
        tiles = x.rearrange("b (t p) d -> p (b t) d", p=P)
        loads = [
            (wa[:], w_qkv.rearrange("(t p) c -> p t c", p=P)), (woa[:], w_out), (wb[:], W_qkv),
            (S["gamma"][:], ln_gamma.unsqueeze(1)), (S["beta"][:], ln_beta.unsqueeze(1)),
            (S["bproj"][:], b_proj.partition_broadcast(P)),
            (S["w1"][:], cn_w1), (S["w2"][:], cn_w2), (S["g1"][:], gc_w1), (S["g2"][:], gc_w2),
            (S["cb1"][:], cn_b1.unsqueeze(1)), (S["gb1"][:], gc_b1.unsqueeze(1)), (S["gb2"][:], gc_b2.unsqueeze(1)),
            (S["g3c"][:], gc_w3), (S["cb4"][:], cn_b4.partition_broadcast(P)),
            (S["gb3"][:], gc_b3.partition_broadcast(P)), (S["ar"][:], adaptive_range.partition_broadcast(P)),
        ]
        for w in range(2):
            for n in range(2):
                c = 2 * D + 64 * n + 32 * w
                loads.append((S["bv"][:, 64 * w + 32 * n:64 * w + 32 * n + 32], b_qkv[c:c + 32].partition_broadcast(P)))
        for s in range(3):
            for n in range(2):
                loads.append((S["bqk"][32 * s:32 * s + 32, n, :], b_qkv[n * D:(n + 1) * D].rearrange("(g r) -> r g", r=GW)))
        for n in range(2):
            loads.append((S["cb2"][64 * n:64 * n + 64, :], cn_b2.unsqueeze(1)))
        for n in range(4):
            loads.append((S["cb3"][32 * n:32 * n + 32, :], cn_b3.unsqueeze(1)))
            loads.append((S["w4c"][32 * n:32 * n + 32, :], cn_w4))
        after_zero = [(S["w3"][0:64, 0:32], cn_w3), (S["w3"][64:128, 32:64], cn_w3)]
        for h in range(H):
            g, i = h // HG, h % HG
            r = 64 * (g // 2) + 16 * i + 8 * (g % 2)
            loads.append((S["wob"][r:r + 8, :], W_proj[8 * h:8 * h + 8, :]))
        NLOAD = len(loads) + len(after_zero)

        @block.sync
        def _(sp):
            for n in range(4):
                sp.dma_start(X[:, 8 * n:8 * n + 8, :], tiles[:, 8 * n:8 * n + 8, :]).then_inc(x_in, 16)
            for dst, src in loads[::2]:
                sp.dma_start(dst, src).then_inc(w_in, 16)
            sp.wait_ge(zeroed, 1)
            for dst, src in after_zero:
                sp.dma_start(dst, src).then_inc(w_in, 16)
            sp.wait_ge(x_in, 64)

        @block.scalar
        def _(act):
            for dst, src in loads[1::2]:
                act.dma_start(dst, src).then_inc(w_in, 16)

        @block.gpsimd
        def _(pool):
            g = nc.gpsimd
            g.memset(S["w3"][:], 0.0).then_inc(zeroed, 1)
            g.memset(S["ident"][:], 0.0)
            g.memset(mask[:], 0.0)
            g.memset(band[:], 1.0)
            g.memset(S["max_row"][:], 0.0)
            g.memset(pickf[:], 0.0)
            g.memset(blocks[:], 1.0)
            g.memset(S["minus_half"][:], -0.5)
            g.memset(S["twist"][:], 0.0).then_inc(zeroed, 1)
            pool.wait_ge(zeroed, 2)
            g.affine_select(out=S["ident"][:], in_=S["ident"][:], compare_op=ALU.not_equal, fill=1.0,
                            base=0, pattern=[[-1, P]], channel_multiplier=1)
            g.affine_select(out=mask[:, 0, :], in_=mask[:, 0, :], compare_op=ALU.is_ge, fill=NEG,
                            base=0, pattern=[[-1, P]], channel_multiplier=1)
            g.affine_select(out=mask[:, 1, :], in_=mask[:, 1, :], compare_op=ALU.is_ge, fill=NEG,
                            base=0, pattern=[[1, P]], channel_multiplier=-1)
            g.affine_select(out=S["max_row"][:], in_=S["max_row"][:], compare_op=ALU.not_equal, fill=1.0,
                            base=-SL, pattern=[[-DH, HG]], channel_multiplier=1)
            g.affine_select(out=pickf[:], in_=pickf[:], compare_op=ALU.not_equal, fill=1.0,
                            base=0, pattern=[[-32, 4], [0, P]], channel_multiplier=1)
            for c0, shift, sign in ((0, 64, 1.0), (32, 64, -1.0), (64, -64, -1.0), (96, -64, 1.0)):
                g.affine_select(out=S["twist"][:, c0:c0 + 32], in_=S["twist"][:, c0:c0 + 32],
                                compare_op=ALU.not_equal, fill=sign, base=-(c0 + shift),
                                pattern=[[-1, 32]], channel_multiplier=1)
            g.affine_select(out=band[:], in_=band[:], compare_op=ALU.is_ge, fill=0.0,
                            base=0, pattern=[[-DH, HG], [-GW, 4]], channel_multiplier=1)
            g.affine_select(out=blocks[:], in_=blocks[:], compare_op=ALU.is_ge, fill=0.0,
                            base=0, pattern=[[-GW, 4], [0, GW]], channel_multiplier=1).then_inc(shaped, 1)
            pool.wait_ge(shaped, 1)
            g.affine_select(out=band[:], in_=band[:], compare_op=ALU.is_ge, fill=0.0,
                            base=DH - 1, pattern=[[DH, HG], [GW, 4]], channel_multiplier=-1)
            g.affine_select(out=blocks[:], in_=blocks[:], compare_op=ALU.is_ge, fill=0.0,
                            base=GW - 1, pattern=[[GW, 4], [0, GW]], channel_multiplier=-1).then_inc(shaped, 1)

        def slots(v):
            return v.rearrange("p (g r) -> p g r", r=GW).unsqueeze(2).broadcast_to([P, G, 3, GW])

        @block.vector
        def _(dve):
            v = nc.vector
            dve.wait_ge(w_in, 16 * NLOAD)
            dve.wait_ge(shaped, 2)
            for n in range(2):
                last = v.tensor_copy(woap[:, 64 * n:64 * n + 64].rearrange("p (i w d) -> p i w d", i=HG, w=2),
                                     woa[:, 64 * n:64 * n + 64].rearrange("p (w i d) -> p i w d", w=2, i=HG))
            last.then_inc(permuted, 1)
            v.tensor_reduce(S["head_rows"][:], band[:], AX, ALU.add)
            v.tensor_copy(S["ident_r"][:], S["ident"][:])
            v.tensor_copy(S["causal_qk"][:], mask[:, 0, :])
            v.tensor_copy(S["causal_kq"][:], mask[:, 1, :])
            v.tensor_copy(S["pick"][:], pickf[:])
            v.tensor_scalar(S["w4"][:], blocks[:].rearrange("p j c -> p (j c)"), S["w4c"][:], None, ALU.mult)
            v.tensor_copy(S["g3"][:], S["g3c"][:].broadcast_to([D // 4, P]))
            v.tensor_scalar(S["ar3"][:], S["ar"][:], 0.3, None, ALU.mult)
            v.tensor_scalar(S["ar7"][:], S["ar"][:], 0.7, None, ALU.mult)
            v.tensor_scalar(S["cb4"][:], S["cb4"][:], 0.5, None, ALU.mult)
            v.tensor_scalar(S["gb3"][:], S["gb3"][:], 0.5, None, ALU.mult)
            for n in range(2):
                v.tensor_copy(S["wqkb"][:, n, :, :].rearrange("p g (s r) -> p g s r", s=3), slots(wb[:, n * D:(n + 1) * D]))
            v.tensor_copy(S["wvb"][:].rearrange("p (w n r) -> p w n r", w=2, n=2),
                          wb[:, 2 * D:3 * D].rearrange("p (n w r) -> p w n r", n=2, w=2))
            dve.wait_ge(turned, 1)
            for n in range(2):
                v.tensor_copy(S["wqka"][:, n, :, :].rearrange("p g (s r) -> p g s r", s=3), slots(ps[:, 0, n * D:(n + 1) * D]))
            v.tensor_copy(S["wva"][:].rearrange("p (w n r) -> p w n r", w=2, n=2),
                          ps[:, 0, 2 * D:3 * D].rearrange("p (n w r) -> p w n r", n=2, w=2))
            v.tensor_copy(S["woa"][:], ps[:, 1, 0:D]).then_inc(made, 1)
            dve.wait_ge(made, 1)

        @block.tensor
        def _(pe):
            pe.wait_ge(w_in, 16 * NLOAD)
            pe.wait_ge(shaped, 2)
            for n in range(3):
                nc.tensor.transpose(ps[:, 0, n * D:(n + 1) * D], wa[:, n, :], S["ident"][:])
            pe.wait_ge(permuted, 1)
            nc.tensor.transpose(ps[:, 1, 0:D], woap[:], S["ident"][:]).then_inc(turned, 1)


def attention(nc, S, ph):
    causal = ph == "a"
    scale = float(np.float32(1) / np.sqrt(DH).astype(np.float32)) if causal else float(DH ** -0.5)
    PW = 384 if causal else 512
    X, ident = S["X"], S["ident"]
    wqk, wv, wo = S["wqk" + ph], S["wv" + ph], S["wo" + ph]
    with ExitStack() as ctx:
        def sb(name, shape, dt=F32):
            return ctx.enter_context(nc.sbuf_tensor(name + "_" + ph, shape, dt))

        def sem(name):
            return ctx.enter_context(nc.semaphore(name + "_" + ph))

        stats = sb("stats", [P, 2, 6])
        mv = sb("mv", [P, 2, 2])
        veps = sb("veps", [P, 2])
        rstd = sb("rstd", [P, 2])
        xn0 = sb("xn0", [P, 2, D])
        xn = sb("xn", [P, 2, D])
        xnT = sb("xnT", [P, 2, T])
        qk = sb("qk", [P, G, 2, T], F32R)
        km = sb("km", [P, G, HG, T], F32R)
        vx = sb("vx", [P, 2, 2, 2 * HG * VB])
        rmax = sb("rmax", [P, 2, HG, 3])
        mw = sb("mw", [P, 2, 2, P])
        probs = sb("probs", [P, HG, 512])
        os_ = sb("os", [P, 2 * T])
        rec = sb("rec", [P, 4 * 2 * HG])
        y = sb("y", [P, 2, D])
        yT = sb("yT", [P, T])
        ps = ctx.enter_context(nc.psum_tensor("ps_" + ph, [P, 8, 512], F32))
        ST = [ps[:, n, :] for n in range(2)]
        MX = [ps[:, 2 + n, :] for n in range(2)]
        O, GEN, TR, TAIL = (ps[:, n, :] for n in range(4, 8))

        xt, vg, gen, mt, mx, st, pv, ot, yt, pj = (sem(n) for n in (
            "xt_b", "vg_b", "gen_u", "mt_u", "mx_h", "st_h", "pv_h", "ot_b", "yt_b", "pj_b"))
        mrow, hi, ex, osb, xnt, ytc = (sem(n) for n in ("mrow_u", "hi_u", "ex_h", "osb_b", "xnt_b", "ytc_b"))
        lo, kmr, red, mr, yn, res, vxr, lnr = (sem(n) for n in (
            "lo_u", "km_u", "red_h", "mr_u", "yn_b", "res_b", "vx_b", "ln_b"))
        ln_step, max_step, rec_step = sem("ln_step"), sem("max_step"), sem("rec_step")
        vepsr, xn0r = sem("veps_n"), sem("xn0_b")
        filled, rsq = sem("filled"), sem("rsqrt_n")
        NORMS = 1 if causal else 2
        REC_STEPS = 1 if causal else 2
        block = ctx.enter_context(nc.Block())

        @block.gpsimd
        def _(pool):
            nc.gpsimd.memset(mw[:], 0.0)
            nc.gpsimd.memset(vx[:], 0.0).then_inc(filled, 1)
            pool.wait_ge(filled, 1)
            for w in range(2):
                ones = vx[:].rearrange("p a t (n e) -> p (a t n) e", e=VB)[:, :, 32 * w + DH:32 * w + DH + 1]
                last = nc.gpsimd.memset(ones, 1.0)
            last.then_inc(filled, 1)

            def inverse_root(b):
                for n in range(NORMS):
                    pool.wait_ge(vepsr, NORMS * b + n + 1)
                    nc.gpsimd.tensor_tensor(rstd[:], veps[:], S["minus_half"][:, 0:2], ALU.pow).then_inc(rsq, 1)

            def add_bias(b):
                pool.wait_ge(res, b + 1)
                t = X[:, bass.ds(2 * b, 2), :]
                nc.gpsimd.tensor_tensor(t, t, S["bproj"][:].unsqueeze(1).broadcast_to([P, 2, D]), ALU.add)

            def batch(b, par, prev, next1, next2):
                if next2:
                    inverse_root(b + 2)
                if prev and not causal:
                    add_bias(b - 1)

            inverse_root(0)
            inverse_root(1)
            over_batches(pool, batch)
            if not causal:
                add_bias(NB - 1)

        @block.tensor
        def _(pe):
            t_ = nc.tensor

            def turn_x(b):
                wait(pe, lnr, b + 1)
                if not (isinstance(b, int) and b == 0):
                    wait(pe, mrow, 4 * b - 3)
                for t in range(2):
                    last = t_.transpose(TR[:, t * P:(t + 1) * P], xn[:, t, :], ident[:])
                last.then_inc(xt, 1)

            def make_v(b, par):
                wait(pe, xnt, b + 1)
                if not (isinstance(b, int) and b == 0):
                    wait(pe, mrow, 4 * b - 1)
                for t in range(2):
                    last = t_.matmul(TR[:, t * P:(t + 1) * P], xnT[:, par, t * P:(t + 1) * P], wv[:], start=True, stop=True)
                last.then_inc(vg, 1)

            def make_qk(b, par, g):
                u = 4 * b + g
                if g == 0:
                    wait(pe, xnt, b + 1)
                wait(pe, lo, u)
                for n in range(2):
                    last = t_.matmul(GEN[0:SL, n * T:(n + 1) * T], wqk[:, n, g, :], xnT[:, par, :], start=True, stop=True)
                last.then_inc(gen, 1)

            def scores_for_max(b, g, heads):
                u = 4 * b + g
                for i in heads:
                    h = 4 * u + i
                    if i == 0:
                        wait(pe, kmr, u + 1)
                    wait(pe, red, h - 1)
                    m, kh = MX[i % 2], km[0:SL, g, i, :]
                    if causal:
                        t_.matmul(m[:, 0:P], qk[0:SL, g, 0, 0:P], kh[:, 0:P], start=True, stop=False)
                        t_.matmul(m[:, 0:P], S["ident_r"][:], S["causal_qk"][:], start=False, stop=True)
                        t_.matmul(m[:, P:3 * P], qk[0:SL, g, 0, P:T], kh, start=True, stop=False)
                        last = t_.matmul(m[:, 2 * P:3 * P], S["ident_r"][:], S["causal_qk"][:], start=False, stop=True)
                    else:
                        for t in range(2):
                            last = t_.matmul(m[:, t * T:(t + 1) * T], qk[0:SL, g, 0, t * P:(t + 1) * P], kh,
                                             start=True, stop=True)
                    last.then_inc(mx, 1)

            def turn_max(b, g, prev, next1):
                u = 4 * b + g
                wait(pe, mr, u + 1)
                if g == 1 and next1:
                    wait(pe, xnt, b + 2)
                elif g == 3 and next1:
                    wait(pe, vxr, b + 2)
                elif g == 0 and not prev:
                    wait(pe, vxr, 1)
                else:
                    wait(pe, mrow, u)
                for t in range(2):
                    last = t_.transpose(TR[:, t * P:(t + 1) * P], mw[:, g % 2, t, :], ident[:])
                last.then_inc(mt, 1)

            def scores(b, g, i):
                h = 16 * b + 4 * g + i
                if i == 0:
                    wait(pe, mrow, 4 * b + g + 1)
                wait(pe, ex, h - 1)
                s, q = ST[i % 2], qk[:, g, 0, :]
                if causal:
                    t_.matmul(s[:, 0:T], km[:, g, i, 0:P], q, start=True, stop=False)
                    t_.matmul(s[:, 0:P], S["ident_r"][:], S["causal_kq"][:], start=False, stop=True)
                    t_.matmul(s[:, T:T + P], km[:, g, i, P:T], q[:, P:T], start=True, stop=False)
                    last = t_.matmul(s[:, T:T + P], S["ident_r"][:], S["causal_kq"][:], start=False, stop=True)
                else:
                    for c in range(2):
                        last = t_.matmul(s[:, c * T:(c + 1) * T], km[:, g, i, c * P:(c + 1) * P], q, start=True, stop=True)
                last.then_inc(st, 1)

            def times_v(b, par, g, i):
                if g == 0 and i == 0:
                    wait(pe, osb, b)
                    wait(pe, vxr, b + 1)
                wait(pe, ex, 16 * b + 4 * g + i + 1)
                w, n = g % 2, g // 2
                for c in range(2):
                    skip = P if causal and c else 0
                    col = (n * HG + i) * VB + 16 * w
                    last = t_.matmul(O[32 * i:32 * i + 32, n * T + skip:(n + 1) * T], vx[:, par, c, col:col + 32],
                                     probs[:, i, c * T:(c + 1) * T - skip], start=(g == 0 and c == 0),
                                     stop=(g == G - 1 and c == 1), skip_group_check=True)
                last.then_inc(pv, 1)

            def turn_o(b):
                wait(pe, osb, b + 1)
                wait(pe, res, b)
                for t in range(2):
                    for n in range(2):
                        last = t_.transpose(TAIL[:, (2 * t + n) * P:(2 * t + n + 1) * P],
                                            os_[:, n * T + t * P:n * T + (t + 1) * P], ident[:])
                last.then_inc(ot, 1)

            def turn_y(b):
                wait(pe, yn, b + 1)
                for t in range(2):
                    last = t_.transpose(TAIL[:, t * P:(t + 1) * P], y[:, t, :], ident[:])
                last.then_inc(yt, 1)

            def project(b):
                wait(pe, ytc, b + 1)
                for t in range(2):
                    last = t_.matmul(TAIL[:, t * P:(t + 1) * P], yT[:, t * P:(t + 1) * P], wo[:], start=True, stop=True)
                last.then_inc(pj, 1)

            def batch(b, par, prev, next1, next2):
                for g in range(G):
                    b1, g1, b2, g2 = b + (g + 1) // G, (g + 1) % G, b + (g + 2) // G, (g + 2) % G
                    ahead1, ahead2 = next1 or g < 3, next1 or g < 2
                    if ahead1:
                        scores_for_max(b1, g1, (0, 1))
                    turn_max(b, g, prev, next1)
                    if ahead2:
                        make_qk(b2, (par + (g + 2) // G) % 2, g2)
                    scores(b, g, 0)
                    scores(b, g, 1)
                    times_v(b, par, g, 0)
                    scores(b, g, 2)
                    times_v(b, par, g, 1)
                    scores(b, g, 3)
                    if ahead1:
                        scores_for_max(b1, g1, (2, 3))
                    times_v(b, par, g, 2)
                    times_v(b, par, g, 3)
                    if g == 0 and next1:
                        turn_x(b + 1)
                    if g == 0 and prev:
                        turn_o(b - 1)
                    if g == 1 and prev:
                        turn_y(b - 1)
                    if g == 2 and prev:
                        project(b - 1)
                    if g == 2 and next1:
                        make_v(b + 1, 1 - par)

            pe.wait_ge(filled, 2)
            turn_x(0)
            make_v(0, 0)
            make_qk(0, 0, 0)
            make_qk(0, 0, 1)
            scores_for_max(0, 0, range(HG))
            over_batches(pe, batch)
            turn_o(NB - 1)
            turn_y(NB - 1)
            project(NB - 1)

        @block.scalar
        def _(act):
            a = nc.scalar

            def copy_xT(b, par):
                act.wait_ge(xt, b + 1)
                if causal:
                    a.activation(xnT[:, par, :], TR[:, 0:T], ACT.Identity).then_inc(xnt, 1)
                else:
                    a.activation(xnT[:, par, :], TR[:, 0:T], ACT.Identity, bias=S["beta"][:],
                                 scale=S["gamma"][:]).then_inc(xnt, 1)

            def high_parts(b, g):
                act.wait_ge(gen, 4 * b + g + 1)
                if causal:
                    a.activation(qk[0:SL, g, :, :].rearrange("p n t -> p (n t)"), GEN[0:SL, :], ACT.Identity).then_inc(hi, 1)
                else:
                    for n in range(2):
                        last = a.activation(qk[0:SL, g, n, :], GEN[0:SL, n * T:(n + 1) * T], ACT.Identity,
                                            bias=S["bqk"][:, n, g:g + 1])
                    last.then_inc(hi, 1)

            def batch(b, par, prev, next1, next2):
                for g in range(G):
                    u = 4 * b + g
                    if g == 0 and prev:
                        act.wait_ge(pv, 16 * b)
                        act.wait_ge(ot, b - 1) if not (isinstance(b, int) and b == 1) else None
                        a.activation(os_[:], O, ACT.Identity).then_inc(osb, 1)
                    act.wait_ge(mt, u + 1)
                    a.activation(qk[SL:P, g, 0, :], TR[SL:P, 0:T], ACT.Identity).then_inc(mrow, 1)
                    if next1 or g < 2:
                        high_parts(b + (g + 2) // G, (g + 2) % G)
                    for i in range(HG):
                        act.wait_ge(st, 4 * u + i + 1)
                        a.activation(probs[:, i, 0:PW], ST[i % 2][:, 0:PW], ACT.Exp, scale=scale).then_inc(ex, 1)
                    if g == 0 and next1:
                        copy_xT(b + 1, 1 - par)
                    if g == 1 and prev:
                        act.wait_ge(yt, b)
                        a.activation(yT[:], TAIL[:, 0:T], ACT.Identity).then_inc(ytc, 1)

            copy_xT(0, 0)
            high_parts(0, 0)
            high_parts(0, 1)
            over_batches(act, batch)
            act.wait_ge(pv, 16 * NB)
            a.activation(os_[:], O, ACT.Identity).then_inc(osb, 1)
            act.wait_ge(yt, NB)
            a.activation(yT[:], TAIL[:, 0:T], ACT.Identity).then_inc(ytc, 1)

        @block.vector
        def _(dve):
            v = nc.vector

            def source(b, k, t):
                return xn0[:, t, :] if k else X[:, bass.ds(2 * b + t, 1), :].rearrange("p a d -> p (a d)")

            def norm_sums(b, k):
                if k:
                    dve.wait_ge(xn0r, b + 1)
                for t in range(2):
                    last = v.bn_stats(stats[:, t, :], source(b, k, t))
                last.then_inc(ln_step, 1)

            def norm_moments(b, k):
                for t in range(2):
                    last = v.bn_aggr(mv[:, t, :], stats[:, t, :])
                last.then_inc(ln_step, 1)
                dve.wait_ge(ln_step, 2 * (NORMS * b + k) + 2)
                v.tensor_scalar(veps[:], mv[:, :, 1], EPS, None, ALU.add).then_inc(vepsr, 1)

            def norm_apply(b, k):
                final = k == NORMS - 1
                dve.wait_ge(rsq, NORMS * b + k + 1)
                if final:
                    wait(dve, xt, b)
                for t in range(2):
                    last = v.tensor_scalar((xn if final else xn0)[:, t, :], source(b, k, t), mv[:, t, 0:1],
                                           rstd[:, t:t + 1], ALU.subtract, ALU.mult)
                last.then_inc(lnr if final else xn0r, 1)

            def layernorm(b):
                for k in range(NORMS):
                    norm_sums(b, k)
                    dve.wait_ge(ln_step, 2 * (NORMS * b + k) + 1)
                    norm_moments(b, k)
                    norm_apply(b, k)

            def copy_v(b, par):
                dve.wait_ge(vg, b + 1)
                for t in range(2):
                    for w in range(2):
                        o = vx[:, par, t, :].rearrange("p (n e) -> p n e", e=VB)[:, :, 32 * w:32 * w + DH]
                        c = t * P + 64 * w
                        i = TR[:, c:c + 64].rearrange("p (n d) -> p n d", d=DH)
                        if causal:
                            last = v.tensor_copy(o, i)
                        else:
                            last = v.tensor_tensor(o, i, S["bv"][:, 64 * w:64 * w + 64].rearrange("p (n d) -> p n d", d=DH), ALU.add)
                last.then_inc(vxr, 1)

            def low_parts(b, g):
                u = 4 * b + g
                dve.wait_ge(hi, u + 1)
                for n, r in ((0, 2 * GW), (1, GW)):
                    part, full = qk[r:r + GW, g, n, :], GEN[r:r + GW, n * T:(n + 1) * T]
                    if causal:
                        last = v.tensor_tensor(part, full, part.bitcast(F32), ALU.subtract)
                    else:
                        last = v.scalar_tensor_tensor(part, full, S["bqk"][r:r + GW, n, g:g + 1], part.bitcast(F32),
                                                      ALU.add, ALU.subtract)
                last.then_inc(lo, 1)
                dve.wait_ge(lo, u + 1)
                for i in range(HG):
                    last = v.tensor_scalar(km[0:SL, g, i, :], qk[0:SL, g, 1, :].bitcast(F32), S["head_rows"][0:SL, i:i + 1],
                                           None, ALU.mult)
                last.then_inc(kmr, 1)

            def maxima(b, g, heads):
                for i in heads:
                    h = 16 * b + 4 * g + i
                    dve.wait_ge(mx, h + 1)
                    if causal:
                        v.reduce_max(rmax[:, g % 2, i, 0:3], MX[i % 2][:, 0:3 * P].rearrange("p (n k) -> p n k", k=P), AX).then_inc(red, 1)
                    else:
                        v.reduce_max(rmax[:, g % 2, i, 0:2], MX[i % 2].rearrange("p (n k) -> p n k", k=T), AX).then_inc(red, 1)

            def spread_maxima(b, g):
                u, r = 4 * b + g, rmax[:, g % 2]
                dve.wait_ge(red, 4 * u + 4)
                wait(dve, mt, u - 1)
                if causal:
                    v.tensor_tensor(r[:, :, 1], r[:, :, 1], r[:, :, 2], ALU.max).then_inc(max_step, 1)
                    dve.wait_ge(max_step, u + 1)
                o = mw[:, g % 2, :, SL:P].rearrange("p t (i e) -> p t i e", e=DH)[:, :, :, 0]
                v.tensor_scalar(o, r[:, :, 0:2].rearrange("p i t -> p t i"), -1.0, None, ALU.mult).then_inc(mr, 1)

            def normalise(b):
                dve.wait_ge(ot, b + 1)
                n = REC_STEPS * b
                o = TAIL.rearrange("p (n e) -> p n e", e=2 * DH)
                if causal:
                    v.reciprocal(rec[:], o[:, :, DH]).then_inc(rec_step, 1)
                    dve.wait_ge(rec_step, n + 1)
                else:
                    v.tensor_scalar(rec[:], o[:, :, DH], 1e-12, None, ALU.max).then_inc(rec_step, 1)
                    dve.wait_ge(rec_step, n + 1)
                    v.reciprocal(rec[:], rec[:]).then_inc(rec_step, 1)
                    dve.wait_ge(rec_step, n + 2)
                wait(dve, yt, b)
                v.tensor_tensor(y[:].rearrange("p t (n d) -> p (t n) d", d=DH), o[:, :, 0:DH],
                                rec[:].unsqueeze(2).broadcast_to([P, 4 * 2 * HG, DH]), ALU.mult).then_inc(yn, 1)

            def add_residual(b):
                dve.wait_ge(pj, b + 1)
                t = X[:, bass.ds(2 * b, 2), :]
                v.tensor_tensor(t, TAIL[:, 0:T].rearrange("p (t d) -> p t d", t=2), t, ALU.add).then_inc(res, 1)

            def batch(b, par, prev, next1, next2):
                for g in range(G):
                    ahead1, ahead2 = next1 or g < 3, next1 or g < 2
                    b1, g1 = b + (g + 1) // G, (g + 1) % G
                    if ahead1:
                        maxima(b1, g1, (0, 1))
                    if ahead2:
                        low_parts(b + (g + 2) // G, (g + 2) % G)
                    norm = {3 - NORMS: 0, 2: NORMS - 1}.get(g) if next2 else None
                    if norm == 1:
                        norm_apply(b + 2, 0)
                    if norm is not None:
                        norm_sums(b + 2, norm)
                        dve.wait_ge(ln_step, 2 * (NORMS * (b + 2) + norm) + 1)
                    if ahead1:
                        maxima(b1, g1, (2, 3))
                    if norm is not None:
                        norm_moments(b + 2, norm)
                    if ahead1:
                        spread_maxima(b1, g1)
                    if g == 0 and prev:
                        normalise(b - 1)
                    if g == 2 and prev:
                        add_residual(b - 1)
                    if g == 2 and next1:
                        copy_v(b + 1, 1 - par)
                    if next2 and g == 3:
                        norm_apply(b + 2, NORMS - 1)

            for g in range(G):
                v.tensor_copy(km[SL:P, g, :, :], S["max_row"][SL:P, :].unsqueeze(2).broadcast_to([P - SL, HG, T]))
            layernorm(0)
            dve.wait_ge(filled, 2)
            copy_v(0, 0)
            low_parts(0, 0)
            low_parts(0, 1)
            maxima(0, 0, range(HG))
            spread_maxima(0, 0)
            layernorm(1)
            over_batches(dve, batch)
            normalise(NB - 1)
            add_residual(NB - 1)


def feed_forward(nc, S, ph, out):
    X, ident = S["X"], S["ident"]
    TT = CH // P
    HB = NCH // 2
    STEPS = 2 * CYCLES
    with ExitStack() as ctx:
        def sb(name, shape, dt=F32):
            return ctx.enter_context(nc.sbuf_tensor(name + "_" + ph, shape, dt))

        def sem(name):
            return ctx.enter_context(nc.semaphore(name + "_" + ph))

        o = sb("o", [P, NCH, CH])
        t = sb("t", [P, NCH, CH])
        xn = sb("xn", [P, 2, TT, D])
        stats = sb("stats", [P, TT, 6])
        mv = sb("mv", [P, 2, TT, 2])
        veps = sb("veps", [P, 2, TT])
        rstd = sb("rstd", [P, 2, TT])
        sums = sb("sums", [P, NB])
        gh1 = sb("gh1", [D // 2, NB])
        gh2 = sb("gh2", [D // 4, NB])
        gate = sb("gate", [P, NB])
        offs = sb("offs", [P, NB])
        off = sb("off", [P, 2, 2])
        h1 = sb("h1", [P, 2, CH])
        h2 = sb("h2", [P, 2, CH])
        h3 = sb("h3", [P, CH])
        th = sb("th", [P, CH])
        c = sb("c", [P, CH])
        chigh = sb("chigh", [P, CH], F32R)
        clow = sb("clow", [P, CH], F32R)
        z_o = sb("z_o", [P, 2, CH])
        z_t = sb("z_t", [P, 2, CH])
        ps = ctx.enter_context(nc.psum_tensor("ps_" + ph, [P, 8, CH], F32))
        H1, H2, BC = [ps[:, n, :] for n in (0, 1)], [ps[:, n, :] for n in (2, 3)], [ps[:, n, :] for n in (4, 5)]
        H3, H4 = ps[:, 6, :], ps[:, 7, :]

        lnr, ln_step, xt, ocp, tw, tcp = (sem(n) for n in ("ln_c", "ln_step", "xt_c", "o_c", "tw_c", "t_c"))
        gmm, gact, goff, off_step = (sem(n) for n in ("gate_mm", "gate_act", "offsets", "off_step"))
        h1m, h2m, h3m, h4m, bcm = (sem(n) for n in ("h1m", "h2m", "h3m", "h4m", "bcm"))
        g1a, g2a, g3a, tha = (sem(n) for n in ("g1a", "g2a", "g3a", "tha"))
        c_step, cr, zr, odone = (sem(n) for n in ("c_step", "c_ready", "z_ready", "o_done"))
        tdone, fin, xdone = sem("t_done"), sem("fin"), sem("x_done")
        vepsr, rsq = sem("veps_c"), sem("rsqrt_c")
        stored = sem("stored")
        block = ctx.enter_context(nc.Block())

        def over_chunks(eng, body):
            for i in range(2):
                body(i, i % 2)
            with eng.Fori(1, NCH // 2) as it:
                body(2 * it, 0)
                body(2 * it + 1, 1)

        @block.tensor
        def _(pe):
            m_ = nc.tensor

            def turn(i, par):
                wait(pe, lnr, i + 1)
                wait(pe, ocp, i - 1)
                for n in range(TT):
                    last = m_.transpose(H1[par][:, n * P:(n + 1) * P], xn[:, par, n, :], ident[:])
                last.then_inc(xt, 1)
                wait(pe, ocp, i + 1)
                wait(pe, tcp, i - 1)
                m_.matmul(H2[par], S["twist"][:], o[:, bass.ds(i, 1), :].rearrange("p a n -> p (a n)"),
                          start=True, stop=True).then_inc(tw, 1)
            over_chunks(pe, turn)

            m_.matmul(H3[0:D // 2, 0:NB], S["g1"][:], sums[:], start=True, stop=True).then_inc(gmm, 1)
            pe.wait_ge(gact, 1)
            m_.matmul(H3[0:D // 4, 0:NB], S["g2"][:], gh1[:], start=True, stop=True).then_inc(gmm, 1)
            pe.wait_ge(gact, 2)
            m_.matmul(H3[:, 0:NB], S["g3"][:], gh2[:], start=True, stop=True).then_inc(gmm, 1)
            pe.wait_ge(gact, 3)
            pe.wait_ge(tcp, NCH)

            def layer1(k, j):
                n = HB * k + j
                wait(pe, odone, HB * (k - 2) + j + 1 if k >= 2 else 0)
                wait(pe, g1a, n - 1)
                m_.matmul(H1[j % 2], S["w1"][:], o[:, HB * (k % 2) + j, :], start=True, stop=True).then_inc(h1m, 1)

            def layer2(k, j):
                n = HB * k + j
                pe.wait_ge(g1a, n + 1)
                if j % 2 == 0:
                    wait(pe, g2a, n // 2 - 1)
                r = 64 * (j % 2)
                m_.matmul(H2[j // 2][r:r + 64, :], S["w2"][:], h1[:, j % 2, :], start=True, stop=True).then_inc(h2m, 1)

            def layer3(k, n):
                pe.wait_ge(g2a, 2 * k + n + 1)
                wait(pe, g3a, k)
                m_.matmul(H3[64 * n:64 * n + 64, :], S["w3"][:], h2[:, n, :], start=True, stop=True).then_inc(h3m, 1)

            def layer4(k):
                pe.wait_ge(g3a, k + 1)
                wait(pe, tha, k)
                m_.matmul(H4, S["w4"][:], h3[:], start=True, stop=True).then_inc(h4m, 1)

            def spread(k, j):
                n = HB * k + j
                if j == 0:
                    pe.wait_ge(cr, k + 1)
                wait(pe, zr, n - 1)
                m_.matmul(BC[j % 2], S["pick"][:, j, :], chigh[:], start=True, stop=False)
                m_.matmul(BC[j % 2], S["pick"][:, j, :], clow[:], start=False, stop=True).then_inc(bcm, 1)

            for k in range(STEPS):
                layer1(k, 0)
                if k:
                    layer3(k - 1, 1)
                layer1(k, 1)
                if k:
                    layer4(k - 1)
                layer2(k, 0)
                layer1(k, 2)
                if k:
                    spread(k - 1, 0)
                layer2(k, 1)
                layer1(k, 3)
                if k:
                    spread(k - 1, 1)
                layer2(k, 2)
                if k:
                    spread(k - 1, 2)
                layer3(k, 0)
                layer2(k, 3)
                if k:
                    spread(k - 1, 3)
            k = STEPS - 1
            layer3(k, 1)
            layer4(k)
            pe.wait_ge(g1a, HB * STEPS)

            def turn_back(n):
                pe.wait_ge(odone, HB * (STEPS - 2) + n + 1)
                wait(pe, xdone, n - 1)
                for q in range(TT):
                    last = m_.transpose(H1[n % 2][:, q * P:(q + 1) * P], o[:, n, q * P:(q + 1) * P], ident[:])
                last.then_inc(fin, 1)
            for j in range(HB):
                turn_back(j)
                spread(k, j)
            for j in range(HB):
                turn_back(HB + j)

        @block.scalar
        def _(act):
            a = nc.scalar

            def copies(i, par):
                act.wait_ge(xt, i + 1)
                for n in range(2):
                    last = a.activation(o[:, bass.ds(i, 1), n * T:(n + 1) * T].rearrange("p a n -> p (a n)"),
                                        H1[par][:, n * T:(n + 1) * T], ACT.Identity,
                                        accum_out=sums[:, bass.ds(2 * i + n, 1)])
                last.then_inc(ocp, 1)
                act.wait_ge(tw, i + 1)
                a.activation(t[:, bass.ds(i, 1), :].rearrange("p a n -> p (a n)"), H2[par], ACT.Identity).then_inc(tcp, 1)
            over_chunks(act, copies)

            act.wait_ge(gmm, 1)
            a.activation(gh1[:], H3[0:D // 2, 0:NB], ACT.Gelu, bias=S["gb1"][:], scale=1.0 / T).then_inc(gact, 1)
            act.wait_ge(gmm, 2)
            a.activation(gh2[:], H3[0:D // 4, 0:NB], ACT.Gelu, bias=S["gb2"][:]).then_inc(gact, 1)
            act.wait_ge(gmm, 3)
            a.activation(gate[:], H3[:, 0:NB], ACT.Tanh, bias=S["gb3"][:], scale=0.5).then_inc(gact, 1)

            def gelu1(k, j):
                n = HB * k + j
                act.wait_ge(h1m, n + 1)
                wait(act, h2m, n - 1)
                a.activation(h1[:, j % 2, :], H1[j % 2], ACT.Gelu, bias=S["cb1"][:]).then_inc(g1a, 1)

            def gelu2(k, n):
                act.wait_ge(h2m, HB * k + 2 * n + 2)
                wait(act, h3m, 2 * k + n - 1)
                a.activation(h2[:, n, :], H2[n], ACT.Gelu, bias=S["cb2"][:]).then_inc(g2a, 1)

            def gelu3(k):
                act.wait_ge(h3m, 2 * k + 2)
                wait(act, h4m, k)
                a.activation(h3[:], H3, ACT.Gelu, bias=S["cb3"][:]).then_inc(g3a, 1)

            def tanh(k):
                act.wait_ge(h4m, k + 1)
                wait(act, cr, k)
                a.activation(th[:], H4, ACT.Tanh, bias=S["cb4"][:], scale=0.5).then_inc(tha, 1)

            for k in range(STEPS):
                gelu1(k, 0)
                if k:
                    gelu2(k - 1, 1)
                    gelu3(k - 1)
                gelu1(k, 1)
                if k:
                    tanh(k - 1)
                gelu1(k, 2)
                gelu1(k, 3)
                gelu2(k, 0)
            k = STEPS - 1
            gelu2(k, 1)
            gelu3(k)
            tanh(k)

        @block.vector
        def _(dve):
            v = nc.vector

            def source(i, n):
                return X[:, bass.ds(TT * i + n, 1), :].rearrange("p a d -> p (a d)")

            def norm_sums(i):
                for n in range(TT):
                    last = v.bn_stats(stats[:, n, :], source(i, n))
                last.then_inc(ln_step, 1)

            def norm_moments(i, par):
                for n in range(TT):
                    last = v.bn_aggr(mv[:, par, n, :], stats[:, n, :])
                last.then_inc(ln_step, 1)
                dve.wait_ge(ln_step, 2 * i + 2)
                v.tensor_scalar(veps[:, par, :], mv[:, par, :, 1], EPS, None, ALU.add).then_inc(vepsr, 1)

            def norm_apply(i, par):
                dve.wait_ge(rsq, i + 1)
                wait(dve, xt, i - 1)
                for n in range(TT):
                    last = v.tensor_scalar(xn[:, par, n, :], source(i, n), mv[:, par, n, 0:1], rstd[:, par, n:n + 1],
                                           ALU.subtract, ALU.mult)
                last.then_inc(lnr, 1)

            def norm(i, par):
                norm_sums(i)
                dve.wait_ge(ln_step, 2 * i + 1)
                if not (isinstance(i, int) and i == 0):
                    norm_apply(i - 1, 1 - par)
                norm_moments(i, par)
            over_chunks(dve, norm)
            norm_apply(NCH - 1, 1)

            dve.wait_ge(gact, 3)
            v.tensor_scalar(offs[:], gate[:], S["ar7"][:], 0.1, ALU.mult, ALU.add).then_inc(off_step, 1)
            dve.wait_ge(off_step, 1)
            for j in range(HB):
                r = slice(32 * j, 32 * j + 32)
                last = v.tensor_copy(off[r, :, :], offs[r, :].rearrange("p (a j h) -> p a j h", a=2, j=HB)[:, :, j, :])
            last.then_inc(goff, 1)
            dve.wait_ge(goff, 1)

            def coupling(k):
                dve.wait_ge(tha, k + 1)
                for n in range(2):
                    last = v.tensor_scalar(c[:, n * T:(n + 1) * T], th[:, n * T:(n + 1) * T], S["ar3"][:],
                                           off[:, k % 2, n:n + 1], ALU.mult, ALU.add)
                last.then_inc(c_step, 1)
                dve.wait_ge(c_step, 2 * k + 1)
                wait(dve, bcm, HB * k)
                v.tensor_copy(chigh[:], c[:]).then_inc(c_step, 1)
                dve.wait_ge(c_step, 2 * k + 2)
                v.tensor_tensor(clow[:], c[:], chigh[:].bitcast(F32), ALU.subtract).then_inc(cr, 1)

            def update(k, j):
                n, q = HB * k + j, HB * (k % 2) + j
                again = k < STEPS - 2
                dve.wait_ge(bcm, n + 1)
                wait(dve, tdone, HB * (k - 2) + j + 1 if k >= 2 else 0)
                z = v.tensor_tensor(z_t[:, j % 2, :], BC[j % 2], t[:, q, :], ALU.mult)
                if again:
                    wait(dve, tdone, n - 1)
                    z = v.tensor_tensor(z_o[:, j % 2, :], BC[j % 2], o[:, q, :], ALU.mult)
                z.then_inc(zr, 1)
                dve.wait_ge(zr, n + 1)
                v.tensor_tensor(o[:, q, :], o[:, q, :], z_t[:, j % 2, :], ALU.add).then_inc(odone, 1)

            dve.wait_ge(tcp, NCH)
            for k in range(1, STEPS):
                coupling(k - 1)
                for j in range(HB):
                    update(k - 1, j)

            def add(n):
                dve.wait_ge(fin, n + 1)
                x = X[:, TT * n:TT * (n + 1), :].rearrange("p a d -> p (a d)")
                v.tensor_tensor(x, H1[n % 2], x, ALU.add).then_inc(xdone, 1)
            k = STEPS - 1
            coupling(k)
            for j in range(HB):
                add(j)
                update(k, j)
            for j in range(HB):
                add(HB + j)

        @block.gpsimd
        def _(pool):
            def inverse_root(i, par):
                pool.wait_ge(vepsr, i + 1)
                nc.gpsimd.tensor_tensor(rstd[:, par, :], veps[:, par, :], S["minus_half"][:, 0:TT], ALU.pow).then_inc(rsq, 1)
            over_chunks(pool, inverse_root)
            for k in range(STEPS - 2):
                for j in range(HB):
                    q = HB * (k % 2) + j
                    pool.wait_ge(zr, HB * k + j + 1)
                    nc.gpsimd.tensor_tensor(t[:, q, :], t[:, q, :], z_o[:, j % 2, :], ALU.subtract).then_inc(tdone, 1)

        if out is not None:
            tiles = out.rearrange("b (t p) d -> p (b t) d", p=P)

            @block.sync
            def _(sp):
                for n in range(NCH):
                    sp.wait_ge(xdone, n + 1)
                    sp.dma_start(tiles[:, TT * n:TT * (n + 1), :], X[:, TT * n:TT * (n + 1), :]).then_inc(stored, 16)
                sp.wait_ge(stored, 16 * NCH)


INPUTS = ["L0_attn_a_x", "L0_attn_a_w_qkv", "L0_attn_a_w_out", "L0_attn_b_ln_gamma", "L0_attn_b_ln_beta",
          "L0_attn_b_W_qkv", "L0_attn_b_b_qkv", "L0_attn_b_W_proj", "L0_attn_b_b_proj",
          "L0_ffn_cn_w1", "L0_ffn_cn_b1", "L0_ffn_cn_w2", "L0_ffn_cn_b2", "L0_ffn_cn_w3", "L0_ffn_cn_b3",
          "L0_ffn_cn_w4", "L0_ffn_cn_b4", "L0_ffn_gc_w1", "L0_ffn_gc_b1", "L0_ffn_gc_w2", "L0_ffn_gc_b2",
          "L0_ffn_gc_w3", "L0_ffn_gc_b3", "L0_ffn_adaptive_range"]


def kernel(**inputs):
    import numpy as _np
    import concourse.bacc as _bacc
    from concourse import mybir as _mybir
    from concourse.bass_utils import run_bass_kernel_spmd as _run

    nc = _bacc.Bacc("TRN2", target_bir_lowering=False, num_devices=1)
    arrays, args = {}, []
    for name in INPUTS:
        a = _np.ascontiguousarray(inputs[name])
        arrays["in_" + name] = a
        args.append(nc.dram_tensor("in_" + name, a.shape, _mybir.dt.from_np(a.dtype), kind="ExternalInput").ap())
    out = nc.dram_tensor("out_x", (NB, T, D), _mybir.dt.float32, kind="ExternalOutput").ap()
    build(nc, *args, out)
    r = _run(nc, [arrays], core_ids=[0])
    return r.results[0]["out_x"]
```

```python
from contextlib import ExitStack

import numpy as np
import concourse.bass as bass
from concourse import mybir
from concourse.alu_op_type import AluOpType as ALU

ACT = mybir.ActivationFunctionType
F32 = mybir.dt.float32
F32R = mybir.dt.float32r
BF16 = mybir.dt.bfloat16
AX = mybir.AxisListType.X

NB, T, D = 16, 256, 128
P = 128
NT = NB * T // P
H, DH = 16, 8
G, HG = 4, 4
GW = HG * DH
SL = 3 * GW
VB = 48
EPS = 1e-5
NEG = -1e30
CH = 512
NCH = NB * T // CH
CYCLES = 3


def wait(eng, sem, value):
    if isinstance(value, int) and value <= 0:
        return
    eng.wait_ge(sem, value)


def over_batches(eng, body):
    for b in (0, 1):
        body(b, b % 2, b, 2)
    with eng.Fori(1, NB // 2 - 1) as it:
        body(2 * it, 0, 2, 2)
        body(2 * it + 1, 1, 2, 2)
    for b in (NB - 2, NB - 1):
        body(b, b % 2, 2, NB - 1 - b)


def build(nc, x, w_qkv, w_out, ln_gamma, ln_beta, W_qkv, b_qkv, W_proj, b_proj,
          cn_w1, cn_b1, cn_w2, cn_b2, cn_w3, cn_b3, cn_w4, cn_b4,
          gc_w1, gc_b1, gc_w2, gc_b2, gc_w3, gc_b3, adaptive_range, out):
    with ExitStack() as ctx:
        def sb(name, shape, dt=F32):
            return ctx.enter_context(nc.sbuf_tensor(name, shape, dt))

        S = {}
        S["X"] = sb("X", [P, NT, D])
        S["ident"] = sb("ident", [P, P])
        S["minus_half"] = sb("minus_half", [P, 4])
        S["ident_h"] = sb("ident_h", [P, P], BF16)
        S["causal_qk"] = sb("causal_qk", [P, 2, P], BF16)
        S["causal_kq"] = sb("causal_kq", [P, 2, P], BF16)
        S["head_rows"] = sb("head_rows", [P, HG])
        S["max_row"] = sb("max_row", [P, HG])
        for ph in "ab":
            S["wqk" + ph] = sb("wqk" + ph, [P, 2, G, SL])
            S["wv" + ph] = sb("wv" + ph, [P, D])
            S["wo" + ph] = sb("wo" + ph, [P, D])
        S["bqk"] = sb("bqk", [P, 2, G])
        S["bv"] = sb("bv", [P, D])
        S["bproj"] = sb("bproj", [P, D])
        S["gamma"] = sb("gamma", [P, 1])
        S["beta"] = sb("beta", [P, 1])
        S["w1"] = sb("w1", [P, D])
        S["w2"] = sb("w2", [P, D // 2])
        S["w3"] = sb("w3", [P, D // 2])
        S["w4"] = sb("w4", [P, P])
        S["w4c"] = sb("w4c", [P, 1])
        S["cb1"] = sb("cb1", [P, 1])
        S["cb2"] = sb("cb2", [P, 1])
        S["cb3"] = sb("cb3", [P, 1])
        S["cb4"] = sb("cb4", [P, 1])
        S["g1"] = sb("g1", [P, D // 2])
        S["g2"] = sb("g2", [D // 2, D // 4])
        S["g3"] = sb("g3", [D // 4, P])
        S["g3c"] = sb("g3c", [D // 4, 1])
        S["gb1"] = sb("gb1", [D // 2, 1])
        S["gb2"] = sb("gb2", [D // 4, 1])
        S["gb3"] = sb("gb3", [P, 1])
        S["ar"] = sb("ar", [P, 1])
        S["ar3"] = sb("ar3", [P, 1])
        S["ar7"] = sb("ar7", [P, 1])
        S["twist"] = sb("twist", [P, P])
        S["pick"] = sb("pick", [P, 4, P], F32R)

        setup(nc, S, x, w_qkv, w_out, ln_gamma, ln_beta, W_qkv, b_qkv, W_proj, b_proj,
              cn_w1, cn_b1, cn_w2, cn_b2, cn_w3, cn_b3, cn_w4, cn_b4,
              gc_w1, gc_b1, gc_w2, gc_b2, gc_w3, gc_b3, adaptive_range)
        attention(nc, S, "a")
        feed_forward(nc, S, "f", None)
        attention(nc, S, "b")
        feed_forward(nc, S, "s", out)


def setup(nc, S, x, w_qkv, w_out, ln_gamma, ln_beta, W_qkv, b_qkv, W_proj, b_proj,
          cn_w1, cn_b1, cn_w2, cn_b2, cn_w3, cn_b3, cn_w4, cn_b4,
          gc_w1, gc_b1, gc_w2, gc_b2, gc_w3, gc_b3, adaptive_range):
    with ExitStack() as ctx:
        wa = ctx.enter_context(nc.sbuf_tensor("set_wa", [P, 3, D], F32))
        woa = ctx.enter_context(nc.sbuf_tensor("set_woa", [P, D], F32))
        woap = ctx.enter_context(nc.sbuf_tensor("woap", [P, D], F32))
        wb = ctx.enter_context(nc.sbuf_tensor("set_wb", [P, 3 * D], F32))
        band = ctx.enter_context(nc.sbuf_tensor("band", [P, HG, 4], F32))
        mask = ctx.enter_context(nc.sbuf_tensor("mask", [P, 2, P], F32))
        pickf = ctx.enter_context(nc.sbuf_tensor("pickf", [P, 4, P], F32))
        blocks = ctx.enter_context(nc.sbuf_tensor("blocks", [P, 4, GW], F32))
        ps = ctx.enter_context(nc.psum_tensor("ps_setup", [P, 2, 512], F32))

        def sem(name):
            return ctx.enter_context(nc.semaphore("set_" + name))
        x_in, w_in = sem("x_in"), sem("w_in")
        zeroed, shaped, made = sem("zeroed"), sem("shaped"), sem("made")
        permuted, turned = sem("permuted"), sem("turned")
        ctx.enter_context(nc.allow_non_contiguous_dma(reason="a few hundred bias values, once"))
        block = ctx.enter_context(nc.Block())
        X = S["X"]
        tiles = x.rearrange("b (t p) d -> p (b t) d", p=P)
        loads = [
            (wa[:], w_qkv.rearrange("(t p) c -> p t c", p=P)), (woa[:], w_out), (wb[:], W_qkv),
            (S["gamma"][:], ln_gamma.unsqueeze(1)), (S["beta"][:], ln_beta.unsqueeze(1)),
            (S["bproj"][:], b_proj.partition_broadcast(P)),
            (S["w1"][:], cn_w1), (S["w2"][:], cn_w2), (S["g1"][:], gc_w1), (S["g2"][:], gc_w2),
            (S["cb1"][:], cn_b1.unsqueeze(1)), (S["gb1"][:], gc_b1.unsqueeze(1)), (S["gb2"][:], gc_b2.unsqueeze(1)),
            (S["g3c"][:], gc_w3), (S["cb4"][:], cn_b4.partition_broadcast(P)),
            (S["gb3"][:], gc_b3.partition_broadcast(P)), (S["ar"][:], adaptive_range.partition_broadcast(P)),
        ]
        for w in range(2):
            for n in range(2):
                c = 2 * D + 64 * n + 32 * w
                loads.append((S["bv"][:, 64 * w + 32 * n:64 * w + 32 * n + 32], b_qkv[c:c + 32].partition_broadcast(P)))
        for n in range(2):
            loads.append((S["cb2"][64 * n:64 * n + 64, :], cn_b2.unsqueeze(1)))
        for n in range(4):
            loads.append((S["cb3"][32 * n:32 * n + 32, :], cn_b3.unsqueeze(1)))
            loads.append((S["w4c"][32 * n:32 * n + 32, :], cn_w4))
        for s in range(3):
            loads.append((S["bqk"][GW * s:GW * s + GW, :, :], b_qkv[0:2 * D].rearrange("(n g r) -> r n g", n=2, g=G)))
        after_zero = [(S["w3"][0:64, 0:32], cn_w3), (S["w3"][64:128, 32:64], cn_w3)]
        for h in range(H):
            g, i = h // HG, h % HG
            r = 64 * (g // 2) + 16 * i + 8 * (g % 2)
            loads.append((S["wob"][r:r + 8, :], W_proj[8 * h:8 * h + 8, :]))
        NLOAD = len(loads) + len(after_zero)

        @block.sync
        def _(sp):
            for n in range(4):
                sp.dma_start(X[:, 8 * n:8 * n + 8, :], tiles[:, 8 * n:8 * n + 8, :]).then_inc(x_in, 16)
            for dst, src in loads[::2]:
                sp.dma_start(dst, src).then_inc(w_in, 16)
            sp.wait_ge(zeroed, 1)
            for dst, src in after_zero:
                sp.dma_start(dst, src).then_inc(w_in, 16)
            sp.wait_ge(x_in, 64)

        @block.scalar
        def _(act):
            for dst, src in loads[1::2]:
                act.dma_start(dst, src).then_inc(w_in, 16)

        @block.gpsimd
        def _(pool):
            g = nc.gpsimd
            g.memset(S["w3"][:], 0.0).then_inc(zeroed, 1)
            g.memset(S["ident"][:], 0.0)
            g.memset(mask[:], 0.0)
            g.memset(band[:], 1.0)
            g.memset(S["max_row"][:], 0.0)
            g.memset(pickf[:], 0.0)
            g.memset(blocks[:], 1.0)
            g.memset(S["minus_half"][:], -0.5)
            g.memset(S["twist"][:], 0.0).then_inc(zeroed, 1)
            pool.wait_ge(zeroed, 2)
            g.affine_select(out=S["ident"][:], in_=S["ident"][:], compare_op=ALU.not_equal, fill=1.0,
                            base=0, pattern=[[-1, P]], channel_multiplier=1)
            g.affine_select(out=mask[:, 0, :], in_=mask[:, 0, :], compare_op=ALU.is_ge, fill=NEG,
                            base=0, pattern=[[-1, P]], channel_multiplier=1)
            g.affine_select(out=mask[:, 1, :], in_=mask[:, 1, :], compare_op=ALU.is_ge, fill=NEG,
                            base=0, pattern=[[1, P]], channel_multiplier=-1)
            g.affine_select(out=S["max_row"][:], in_=S["max_row"][:], compare_op=ALU.not_equal, fill=1.0,
                            base=-SL, pattern=[[-DH, HG]], channel_multiplier=1)
            g.affine_select(out=pickf[:], in_=pickf[:], compare_op=ALU.not_equal, fill=1.0,
                            base=0, pattern=[[-32, 4], [0, P]], channel_multiplier=1)
            for c0, shift, sign in ((0, 64, 1.0), (32, 64, -1.0), (64, -64, -1.0), (96, -64, 1.0)):
                g.affine_select(out=S["twist"][:, c0:c0 + 32], in_=S["twist"][:, c0:c0 + 32],
                                compare_op=ALU.not_equal, fill=sign, base=-(c0 + shift),
                                pattern=[[-1, 32]], channel_multiplier=1)
            g.affine_select(out=band[:], in_=band[:], compare_op=ALU.is_ge, fill=0.0,
                            base=0, pattern=[[-DH, HG], [-GW, 4]], channel_multiplier=1)
            g.affine_select(out=blocks[:], in_=blocks[:], compare_op=ALU.is_ge, fill=0.0,
                            base=0, pattern=[[-GW, 4], [0, GW]], channel_multiplier=1).then_inc(shaped, 1)
            pool.wait_ge(shaped, 1)
            g.affine_select(out=band[:], in_=band[:], compare_op=ALU.is_ge, fill=0.0,
                            base=DH - 1, pattern=[[DH, HG], [GW, 4]], channel_multiplier=-1)
            g.affine_select(out=blocks[:], in_=blocks[:], compare_op=ALU.is_ge, fill=0.0,
                            base=GW - 1, pattern=[[GW, 4], [0, GW]], channel_multiplier=-1).then_inc(shaped, 1)

        def slots(v):
            return v.rearrange("p (g r) -> p g r", r=GW).unsqueeze(2).broadcast_to([v.shape[0], G, 3, GW])

        @block.vector
        def _(dve):
            v = nc.vector
            dve.wait_ge(w_in, 16 * NLOAD)
            dve.wait_ge(shaped, 2)
            for n in range(2):
                last = v.tensor_copy(woap[:, 64 * n:64 * n + 64].rearrange("p (i w d) -> p i w d", i=HG, w=2),
                                     woa[:, 64 * n:64 * n + 64].rearrange("p (w i d) -> p i w d", w=2, i=HG))
            last.then_inc(permuted, 1)
            v.tensor_reduce(S["head_rows"][:], band[:], AX, ALU.add)
            v.tensor_copy(S["ident_h"][:], S["ident"][:])
            v.tensor_copy(S["causal_qk"][:], mask[:, 0, :].unsqueeze(1).broadcast_to([P, 2, P]))
            v.tensor_copy(S["causal_kq"][:], mask[:, 1, :].unsqueeze(1).broadcast_to([P, 2, P]))
            v.tensor_copy(S["pick"][:], pickf[:])
            v.tensor_scalar(S["w4"][:], blocks[:].rearrange("p j c -> p (j c)"), S["w4c"][:], None, ALU.mult)
            v.tensor_copy(S["g3"][:], S["g3c"][:].broadcast_to([D // 4, P]))
            v.tensor_scalar(S["ar3"][:], S["ar"][:], 0.3, None, ALU.mult)
            v.tensor_scalar(S["ar7"][:], S["ar"][:], 0.7, None, ALU.mult)
            v.tensor_scalar(S["cb4"][:], S["cb4"][:], 0.5, None, ALU.mult)
            v.tensor_scalar(S["gb3"][:], S["gb3"][:], 0.5, None, ALU.mult)
            for n in range(2):
                v.tensor_copy(S["wqkb"][:, n, :, :].rearrange("p g (s r) -> p g s r", s=3), slots(wb[:, n * D:(n + 1) * D]))
            v.tensor_copy(S["wvb"][:].rearrange("p (w n r) -> p w n r", w=2, n=2),
                          wb[:, 2 * D:3 * D].rearrange("p (n w r) -> p w n r", n=2, w=2))
            dve.wait_ge(turned, 1)
            for n in range(2):
                v.tensor_copy(S["wqka"][:, n, :, :].rearrange("p g (s r) -> p g s r", s=3), slots(ps[:, 0, n * D:(n + 1) * D]))
            v.tensor_copy(S["wva"][:].rearrange("p (w n r) -> p w n r", w=2, n=2),
                          ps[:, 0, 2 * D:3 * D].rearrange("p (n w r) -> p w n r", n=2, w=2))
            v.tensor_copy(S["woa"][:], ps[:, 1, 0:D]).then_inc(made, 1)
            dve.wait_ge(made, 1)

        @block.tensor
        def _(pe):
            pe.wait_ge(w_in, 16 * NLOAD)
            pe.wait_ge(shaped, 2)
            for n in range(3):
                nc.tensor.transpose(ps[:, 0, n * D:(n + 1) * D], wa[:, n, :], S["ident"][:])
            pe.wait_ge(permuted, 1)
            nc.tensor.transpose(ps[:, 1, 0:D], woap[:], S["ident"][:]).then_inc(turned, 1)


def attention(nc, S, ph):
    causal = ph == "a"
    scale = float(np.float32(1) / np.sqrt(DH).astype(np.float32)) if causal else float(DH ** -0.5)
    PW = 384 if causal else 512
    X, ident = S["X"], S["ident"]
    wqk, wv, wo = S["wqk" + ph], S["wv" + ph], S["wo" + ph]
    with ExitStack() as ctx:
        def sb(name, shape, dt=F32):
            return ctx.enter_context(nc.sbuf_tensor(name + "_" + ph, shape, dt))

        def sem(name):
            return ctx.enter_context(nc.semaphore(name + "_" + ph))

        stats = sb("stats", [P, 2, 6])
        mv = sb("mv", [P, 2, 2])
        veps = sb("veps", [P, 2])
        rstd = sb("rstd", [P, 2])
        centred = sb("centred", [P, 2, D])
        xn0 = sb("xn0", [P, 2, D])
        xn = sb("xn", [P, 2, D])
        xnT = sb("xnT", [P, 2, T])
        qk = sb("qk", [P, G, 2, T], F32R)
        km = sb("km", [P, G, HG, T], F32R)
        vx = sb("vx", [P, 2, 2, 2 * HG * VB])
        rmax = sb("rmax", [P, 2, HG, 3])
        mw = sb("mw", [P, 2, 2, P])
        probs = sb("probs", [P, 2, HG, 512])
        os_ = sb("os", [P, 2 * T])
        rec = sb("rec", [P, 4 * 2 * HG])
        y = sb("y", [P, 2, D])
        yT = sb("yT", [P, T])
        ps = ctx.enter_context(nc.psum_tensor("ps_" + ph, [P, 8, 512], F32))
        ST = [ps[:, n, :] for n in range(2)]
        MX = [ps[:, 2 + n, :] for n in range(2)]
        O, GEN, TR, TAIL = (ps[:, n, :] for n in range(4, 8))

        xt, vg, gen, mt, mx, st, pv, ot, yt, pj = (sem(n) for n in (
            "xt_b", "vg_b", "gen_u", "mt_u", "mx_h", "st_h", "pv_u", "ot_b", "yt_b", "pj_b"))
        mrow, hi, kmr2, ex, osb, xnt, ytc = (sem(n) for n in ("mrow_u", "hi_u", "km2_u", "ex_h", "osb_b", "xnt_b", "ytc_b"))
        lo, red, mr, yn, res, vxr, lnr = (sem(n) for n in (
            "lo_u", "red_h", "mr_u", "yn_b", "res_b", "vx_b", "ln_b"))
        ln_step, max_step, rec_step = sem("ln_step"), sem("max_step"), sem("rec_step")
        vepsr, xn0r = sem("veps_n"), sem("xn0_b")
        filled, rsq, kmr = sem("filled"), sem("rsqrt_n"), sem("km_u")
        NORMS = 1 if causal else 2
        REC_STEPS = 1 if causal else 2
        block = ctx.enter_context(nc.Block())

        @block.gpsimd
        def _(pool):
            nc.gpsimd.memset(mw[:], 0.0)
            nc.gpsimd.memset(vx[:], 0.0).then_inc(filled, 1)
            pool.wait_ge(filled, 1)
            for w in range(2):
                ones = vx[:].rearrange("p a t (n e) -> p (a t n) e", e=VB)[:, :, 32 * w + DH:32 * w + DH + 1]
                last = nc.gpsimd.memset(ones, 1.0)
            last.then_inc(filled, 1)

            def norm(b, k):
                n, final = NORMS * b + k, k == NORMS - 1
                pool.wait_ge(vepsr, n + 1)
                nc.gpsimd.tensor_tensor(rstd[:], veps[:], S["minus_half"][:, 0:2], ALU.pow)
                src = xn0[:] if k else X[:, bass.ds(2 * b, 2), :]
                mean = mv[:, :, 0].unsqueeze(2).broadcast_to([P, 2, D])
                nc.gpsimd.tensor_tensor(centred[:], src, mean, ALU.subtract).then_inc(rsq, 1)
                pool.wait_ge(rsq, n + 1)
                if final:
                    wait(pool, xt, b)
                nc.gpsimd.tensor_tensor((xn if final else xn0)[:], centred[:], rstd[:].unsqueeze(2).broadcast_to([P, 2, D]),
                                        ALU.mult).then_inc(lnr if final else xn0r, 1)

            def mask_k(b, g):
                pool.wait_ge(lo, 4 * b + g + 1)
                nc.gpsimd.tensor_tensor(km[0:SL, g, 0:2, :], qk[0:SL, g, 1, :].bitcast(F32).unsqueeze(1).broadcast_to([SL, 2, T]),
                                        S["head_rows"][0:SL, 0:2].unsqueeze(2).broadcast_to([SL, 2, T]),
                                        ALU.mult).then_inc(kmr, 1)

            def add_bias(b):
                pool.wait_ge(res, b + 1)
                t = X[:, bass.ds(2 * b, 2), :]
                nc.gpsimd.tensor_tensor(t, t, S["bproj"][:].unsqueeze(1).broadcast_to([P, 2, D]), ALU.add)

            def batch(b, par, behind, ahead):
                for g in range(G):
                    b3, g3 = b + (g + 3) // G, (g + 3) % G
                    if ahead or g < 1:
                        mask_k(b3, g3)
                    if ahead == 2 and g >= G - 1 - NORMS and g < G - 1:
                        norm(b + 2, g - (G - 1 - NORMS))
                    if behind == 2 and g == 0 and not causal:
                        add_bias(b - 2)

            for k in range(NORMS):
                norm(0, k)
            for g in range(3):
                mask_k(0, g)
            for k in range(NORMS):
                norm(1, k)
            over_batches(pool, batch)
            if not causal:
                add_bias(NB - 2)
                add_bias(NB - 1)

        @block.tensor
        def _(pe):
            t_ = nc.tensor

            def diagonal(bank):
                return bank.rearrange("p (n a k) -> p n a k", n=2, a=2)[:, :, 0, :]

            def turn_x(b):
                wait(pe, lnr, b + 1)
                wait(pe, res, b - 2)
                wait(pe, vxr, b)
                for t in range(2):
                    last = t_.transpose(TAIL[:, t * P:(t + 1) * P], xn[:, t, :], ident[:])
                last.then_inc(xt, 1)

            def make_v(b, par):
                wait(pe, xnt, b + 1)
                wait(pe, ytc, b - 1)
                for t in range(2):
                    last = t_.matmul(TAIL[:, t * P:(t + 1) * P], xnT[:, par, t * P:(t + 1) * P], wv[:], start=True, stop=True)
                last.then_inc(vg, 1)

            def make_qk(b, par, g):
                u = 4 * b + g
                if g == 0:
                    wait(pe, xnt, b + 1)
                wait(pe, lo, u)
                for n in range(2):
                    last = t_.matmul(GEN[0:SL, n * T:(n + 1) * T], wqk[:, n, g, :], xnT[:, par, :], start=True, stop=True)
                last.then_inc(gen, 1)

            def scores_for_max(b, g, heads):
                u = 4 * b + g
                for i in heads:
                    h = 4 * u + i
                    if i == 0:
                        wait(pe, kmr, u + 1)
                    if i == 2:
                        wait(pe, kmr2, u + 1)
                    wait(pe, red, h - 1)
                    m, kh = MX[i % 2], km[0:SL, g, i, :]
                    if causal:
                        t_.matmul(m[:, 0:P], qk[0:SL, g, 0, 0:P], kh[:, 0:P], start=True, stop=True)
                        t_.matmul(m[:, P:3 * P], qk[0:SL, g, 0, P:T], kh, start=False, stop=True, skip_group_check=True)
                        last = t_.matmul(diagonal(m), S["ident_h"][:], S["causal_qk"][:], start=False, stop=True,
                                         skip_group_check=True)
                    else:
                        for t in range(2):
                            last = t_.matmul(m[:, t * T:(t + 1) * T], qk[0:SL, g, 0, t * P:(t + 1) * P], kh,
                                             start=True, stop=True)
                    last.then_inc(mx, 1)

            def turn_max(b, g):
                u = 4 * b + g
                wait(pe, mr, u + 1)
                wait(pe, mrow, u)
                for t in range(2):
                    last = t_.transpose(TR[:, t * P:(t + 1) * P], mw[:, g % 2, t, :], ident[:])
                last.then_inc(mt, 1)

            def scores(b, g, i):
                h = 16 * b + 4 * g + i
                if i == 0:
                    wait(pe, mrow, 4 * b + g + 1)
                wait(pe, ex, h - 1)
                s, q = ST[i % 2], qk[:, g, 0, :]
                if causal:
                    t_.matmul(s[:, T:3 * P], km[:, g, i, P:T], q[:, P:T], start=True, stop=True)
                    t_.matmul(s[:, 0:T], km[:, g, i, 0:P], q, start=False, stop=True, skip_group_check=True)
                    last = t_.matmul(diagonal(s), S["ident_h"][:], S["causal_kq"][:], start=False, stop=True,
                                     skip_group_check=True)
                else:
                    for c in range(2):
                        last = t_.matmul(s[:, c * T:(c + 1) * T], km[:, g, i, c * P:(c + 1) * P], q, start=True, stop=True)
                last.then_inc(st, 1)

            def times_v(b, par, g):
                if g == 0:
                    wait(pe, osb, b)
                    wait(pe, vxr, b + 1)
                wait(pe, ex, 16 * b + 4 * g + 4)
                w, n = g % 2, g // 2
                for c in range(2):
                    for i in range(HG):
                        skip = P if causal and c else 0
                        col = (n * HG + i) * VB + 16 * w
                        last = t_.matmul(O[32 * i:32 * i + 32, n * T + skip:(n + 1) * T], vx[:, par, c, col:col + 32],
                                         probs[:, g % 2, i, c * T:(c + 1) * T - skip], start=(g == 0 and c == 0),
                                         stop=(g == G - 1 and c == 1), skip_group_check=True)
                last.then_inc(pv, 1)

            def turn_o(b, has_x):
                wait(pe, osb, b + 1)
                wait(pe, res, b)
                if has_x:
                    pe.wait_ge(xnt, b + 3)
                for t in range(2):
                    for n in range(2):
                        last = t_.transpose(TAIL[:, (2 * t + n) * P:(2 * t + n + 1) * P],
                                            os_[:, n * T + t * P:n * T + (t + 1) * P], ident[:])
                last.then_inc(ot, 1)

            def turn_y(b):
                wait(pe, yn, b + 1)
                for t in range(2):
                    last = t_.transpose(TAIL[:, t * P:(t + 1) * P], y[:, t, :], ident[:])
                last.then_inc(yt, 1)

            def project(b, has_v):
                wait(pe, ytc, b + 1)
                if has_v:
                    pe.wait_ge(vxr, b + 3)
                for t in range(2):
                    last = t_.matmul(TAIL[:, t * P:(t + 1) * P], yT[:, t * P:(t + 1) * P], wo[:], start=True, stop=True)
                last.then_inc(pj, 1)

            def batch(b, par, behind, ahead):
                more = ahead > 0
                for g in range(G):
                    (b1, g1), (b2, g2), (b3, g3) = ((b + (g + n) // G, (g + n) % G) for n in (1, 2, 3))
                    if more or g < 1:
                        make_qk(b3, (par + (g + 3) // G) % 2, g3)
                    scores(b, g, 0)
                    scores(b, g, 1)
                    if more and g == 0:
                        turn_x(b + 1)
                    if more or g < 2:
                        scores_for_max(b2, g2, (0, 1))
                    if g:
                        times_v(b, par, g - 1)
                    elif behind:
                        times_v(b - 1, 1 - par, G - 1)
                    if more or g < 3:
                        turn_max(b1, g1)
                    if behind and g == 1:
                        turn_o(b - 1, more)
                    if behind and g == 2:
                        turn_y(b - 1)
                    if more or g < 2:
                        scores_for_max(b2, g2, (2,))
                    scores(b, g, 2)
                    if more or g < 2:
                        scores_for_max(b2, g2, (3,))
                    scores(b, g, 3)
                    if more and g == 2:
                        make_v(b + 1, 1 - par)
                    if behind and g == 3:
                        project(b - 1, more)

            pe.wait_ge(filled, 2)
            turn_x(0)
            make_v(0, 0)
            make_qk(0, 0, 0)
            make_qk(0, 0, 1)
            scores_for_max(0, 0, range(HG))
            turn_max(0, 0)
            make_qk(0, 0, 2)
            scores_for_max(0, 1, range(HG))
            over_batches(pe, batch)
            times_v(NB - 1, 1, G - 1)
            turn_o(NB - 1, False)
            turn_y(NB - 1)
            project(NB - 1, False)

        @block.scalar
        def _(act):
            a = nc.scalar

            def copy_xT(b, par):
                act.wait_ge(xt, b + 1)
                if causal:
                    a.activation(xnT[:, par, :], TAIL[:, 0:T], ACT.Identity).then_inc(xnt, 1)
                else:
                    a.activation(xnT[:, par, :], TAIL[:, 0:T], ACT.Identity, bias=S["beta"][:],
                                 scale=S["gamma"][:]).then_inc(xnt, 1)

            def high_parts(b, g):
                act.wait_ge(gen, 4 * b + g + 1)
                if causal:
                    a.activation(qk[0:SL, g, :, :].rearrange("p n t -> p (n t)"), GEN[0:SL, :], ACT.Identity).then_inc(hi, 1)
                else:
                    for n in range(2):
                        last = a.activation(qk[0:SL, g, n, :], GEN[0:SL, n * T:(n + 1) * T], ACT.Identity,
                                            bias=S["bqk"][0:SL, n, g:g + 1])
                    last.then_inc(hi, 1)

            def mask_k(b, g):
                act.wait_ge(lo, 4 * b + g + 1)
                for i in (2, 3):
                    last = a.activation(km[0:SL, g, i, :], qk[0:SL, g, 1, :].bitcast(F32), ACT.Copy,
                                        scale=S["head_rows"][0:SL, i:i + 1])
                last.then_inc(kmr2, 1)

            def max_row(b, g):
                act.wait_ge(mt, 4 * b + g + 1)
                a.activation(qk[SL:P, g, 0, :], TR[SL:P, 0:T], ACT.Identity).then_inc(mrow, 1)

            def exponentials(b, g, i):
                act.wait_ge(st, 16 * b + 4 * g + i + 1)
                a.activation(probs[:, g % 2, i, 0:PW], ST[i % 2][:, 0:PW], ACT.Exp, scale=scale).then_inc(ex, 1)

            def copy_o(b):
                act.wait_ge(pv, 4 * b + 4)
                wait(act, ot, b)
                a.activation(os_[:], O, ACT.Identity).then_inc(osb, 1)

            def copy_yT(b):
                act.wait_ge(yt, b + 1)
                wait(act, pj, b)
                a.activation(yT[:], TAIL[:, 0:T], ACT.Identity).then_inc(ytc, 1)

            def batch(b, par, behind, ahead):
                more = ahead > 0
                for g in range(G):
                    (b1, g1), (b3, g3) = ((b + (g + n) // G, (g + n) % G) for n in (1, 3))
                    if more or g < 1:
                        high_parts(b3, g3)
                    exponentials(b, g, 0)
                    exponentials(b, g, 1)
                    if more and g == 0:
                        copy_xT(b + 1, 1 - par)
                    if behind and g == 0:
                        copy_o(b - 1)
                    if more or g < 3:
                        max_row(b1, g1)
                    if behind and g == 2:
                        copy_yT(b - 1)
                    exponentials(b, g, 2)
                    exponentials(b, g, 3)
                    if more or g < 1:
                        mask_k(b3, g3)

            copy_xT(0, 0)
            high_parts(0, 0)
            mask_k(0, 0)
            high_parts(0, 1)
            mask_k(0, 1)
            max_row(0, 0)
            high_parts(0, 2)
            mask_k(0, 2)
            over_batches(act, batch)
            copy_o(NB - 1)
            copy_yT(NB - 1)

        @block.vector
        def _(dve):
            v = nc.vector

            def source(b, k, t):
                return xn0[:, t, :] if k else X[:, bass.ds(2 * b + t, 1), :].rearrange("p a d -> p (a d)")

            def norm_sums(b, k):
                if k:
                    dve.wait_ge(xn0r, b + 1)
                else:
                    wait(dve, lnr, b)
                for t in range(2):
                    last = v.bn_stats(stats[:, t, :], source(b, k, t))
                last.then_inc(ln_step, 1)

            def norm_moments(b, k):
                for t in range(2):
                    last = v.bn_aggr(mv[:, t, :], stats[:, t, :])
                last.then_inc(ln_step, 1)
                dve.wait_ge(ln_step, 2 * (NORMS * b + k) + 2)
                v.tensor_scalar(veps[:], mv[:, :, 1], EPS, None, ALU.add).then_inc(vepsr, 1)

            def layernorm(b):
                for k in range(NORMS):
                    norm_sums(b, k)
                    dve.wait_ge(ln_step, 2 * (NORMS * b + k) + 1)
                    norm_moments(b, k)

            def copy_v(b, par):
                dve.wait_ge(vg, b + 1)
                for w in range(2):
                    o = vx[:, par, :, :].rearrange("p t (n e) -> p t n e", e=VB)[:, :, :, 32 * w:32 * w + DH]
                    i = TAIL[:, 0:T].rearrange("p (t w n d) -> p t w n d", t=2, w=2, d=DH)[:, :, w]
                    if causal:
                        last = v.tensor_copy(o, i)
                    else:
                        bv = S["bv"][:, 64 * w:64 * w + 64].rearrange("p (n d) -> p n d", d=DH)
                        last = v.tensor_tensor(o, i, bv.unsqueeze(1).broadcast_to([P, 2, 2 * HG, DH]), ALU.add)
                last.then_inc(vxr, 1)

            def low_parts(b, g):
                u = 4 * b + g
                dve.wait_ge(hi, u + 1)
                for n, r in ((0, 2 * GW), (1, GW)):
                    part, full = qk[r:r + GW, g, n, :], GEN[r:r + GW, n * T:(n + 1) * T]
                    if causal:
                        last = v.tensor_tensor(part, full, part.bitcast(F32), ALU.subtract)
                    else:
                        last = v.scalar_tensor_tensor(part, full, S["bqk"][r:r + GW, n, g:g + 1], part.bitcast(F32),
                                                      ALU.add, ALU.subtract)
                last.then_inc(lo, 1)
            def maxima(b, g, heads):
                for i in heads:
                    h = 16 * b + 4 * g + i
                    dve.wait_ge(mx, h + 1)
                    if causal:
                        v.reduce_max(rmax[:, g % 2, i, 0:3], MX[i % 2][:, 0:3 * P].rearrange("p (n k) -> p n k", k=P), AX).then_inc(red, 1)
                    else:
                        v.reduce_max(rmax[:, g % 2, i, 0:2], MX[i % 2].rearrange("p (n k) -> p n k", k=T), AX).then_inc(red, 1)

            def spread_maxima(b, g):
                u, r = 4 * b + g, rmax[:, g % 2]
                dve.wait_ge(red, 4 * u + 4)
                wait(dve, mt, u - 1)
                if causal:
                    v.tensor_tensor(r[:, :, 1], r[:, :, 1], r[:, :, 2], ALU.max).then_inc(max_step, 1)
                    dve.wait_ge(max_step, u + 1)
                o = mw[:, g % 2, :, SL:P].rearrange("p t (i e) -> p t i e", e=DH)[:, :, :, 0]
                v.tensor_scalar(o, r[:, :, 0:2].rearrange("p i t -> p t i"), -1.0, None, ALU.mult).then_inc(mr, 1)

            def normalise(b):
                dve.wait_ge(ot, b + 1)
                n = REC_STEPS * b
                o = TAIL.rearrange("p (n e) -> p n e", e=2 * DH)
                if causal:
                    v.reciprocal(rec[:], o[:, :, DH]).then_inc(rec_step, 1)
                    dve.wait_ge(rec_step, n + 1)
                else:
                    v.tensor_scalar(rec[:], o[:, :, DH], 1e-12, None, ALU.max).then_inc(rec_step, 1)
                    dve.wait_ge(rec_step, n + 1)
                    v.reciprocal(rec[:], rec[:]).then_inc(rec_step, 1)
                    dve.wait_ge(rec_step, n + 2)
                wait(dve, yt, b)
                v.tensor_tensor(y[:].rearrange("p t (n d) -> p (t n) d", d=DH), o[:, :, 0:DH],
                                rec[:].unsqueeze(2).broadcast_to([P, 4 * 2 * HG, DH]), ALU.mult).then_inc(yn, 1)

            def add_residual(b):
                dve.wait_ge(pj, b + 1)
                t = X[:, bass.ds(2 * b, 2), :]
                v.tensor_tensor(t, TAIL[:, 0:T].rearrange("p (t d) -> p t d", t=2), t, ALU.add).then_inc(res, 1)

            def batch(b, par, behind, ahead):
                more = ahead > 0
                for g in range(G):
                    (b2, g2), (b3, g3) = ((b + (g + n) // G, (g + n) % G) for n in (2, 3))
                    if behind == 2 and g == 0:
                        add_residual(b - 2)
                    if more or g < 2:
                        maxima(b2, g2, (0, 1))
                    if more or g < 1:
                        low_parts(b3, g3)
                    if behind and g == 1:
                        normalise(b - 1)
                    if more and g == 3:
                        copy_v(b + 1, 1 - par)
                    norm = {3 - NORMS: 0, 2: NORMS - 1}.get(g) if ahead == 2 else None
                    if norm is not None:
                        norm_sums(b + 2, norm)
                        dve.wait_ge(ln_step, 2 * (NORMS * (b + 2) + norm) + 1)
                    if more or g < 2:
                        maxima(b2, g2, (2, 3))
                    if norm is not None:
                        norm_moments(b + 2, norm)
                    if more or g < 2:
                        spread_maxima(b2, g2)

            for g in range(G):
                v.tensor_copy(km[SL:P, g, :, :], S["max_row"][SL:P, :].unsqueeze(2).broadcast_to([P - SL, HG, T]))
            layernorm(0)
            dve.wait_ge(filled, 2)
            copy_v(0, 0)
            low_parts(0, 0)
            low_parts(0, 1)
            maxima(0, 0, range(HG))
            spread_maxima(0, 0)
            low_parts(0, 2)
            maxima(0, 1, range(HG))
            spread_maxima(0, 1)
            layernorm(1)
            over_batches(dve, batch)
            add_residual(NB - 2)
            normalise(NB - 1)
            add_residual(NB - 1)


def feed_forward(nc, S, ph, out):
    X, ident = S["X"], S["ident"]
    TT = CH // P
    HB = NCH // 2
    STEPS = 2 * CYCLES
    with ExitStack() as ctx:
        def sb(name, shape, dt=F32):
            return ctx.enter_context(nc.sbuf_tensor(name + "_" + ph, shape, dt))

        def sem(name):
            return ctx.enter_context(nc.semaphore(name + "_" + ph))

        o = sb("o", [P, NCH, CH])
        t = sb("t", [P, NCH, CH])
        xn = sb("xn", [P, 2, TT, D])
        stats = sb("stats", [P, TT, 6])
        mv = sb("mv", [P, 2, TT, 2])
        veps = sb("veps", [P, 2, TT])
        rstd = sb("rstd", [P, 2, TT])
        sums = sb("sums", [P, NB])
        gh1 = sb("gh1", [D // 2, NB])
        gh2 = sb("gh2", [D // 4, NB])
        gate = sb("gate", [P, NB])
        offs = sb("offs", [P, NB])
        off = sb("off", [P, 2, 2])
        h1 = sb("h1", [P, 2, CH])
        h2 = sb("h2", [P, 2, CH])
        h3 = sb("h3", [P, CH])
        th = sb("th", [P, CH])
        c = sb("c", [P, CH])
        chigh = sb("chigh", [P, CH], F32R)
        clow = sb("clow", [P, CH], F32R)
        z_o = sb("z_o", [P, 2, CH])
        z_t = sb("z_t", [P, 2, CH])
        ps = ctx.enter_context(nc.psum_tensor("ps_" + ph, [P, 8, CH], F32))
        H1, H2, BC = [ps[:, n, :] for n in (0, 1)], [ps[:, n, :] for n in (2, 3)], [ps[:, n, :] for n in (4, 5)]
        H3, H4 = ps[:, 6, :], ps[:, 7, :]

        lnr, ln_step, xt, ocp, tw, tcp = (sem(n) for n in ("ln_c", "ln_step", "xt_c", "o_c", "tw_c", "t_c"))
        gmm, gact, goff, off_step = (sem(n) for n in ("gate_mm", "gate_act", "offsets", "off_step"))
        h1m, h2m, h3m, h4m, bcm = (sem(n) for n in ("h1m", "h2m", "h3m", "h4m", "bcm"))
        g1a, g2a, g3a, tha = (sem(n) for n in ("g1a", "g2a", "g3a", "tha"))
        c_step, cr, zr, odone = (sem(n) for n in ("c_step", "c_ready", "z_ready", "o_done"))
        tdone, fin, xdone = sem("t_done"), sem("fin"), sem("x_done")
        vepsr, rsq = sem("veps_c"), sem("rsqrt_c")
        stored = sem("stored")
        block = ctx.enter_context(nc.Block())

        def over_chunks(eng, body):
            for i in range(2):
                body(i, i % 2)
            with eng.Fori(1, NCH // 2) as it:
                body(2 * it, 0)
                body(2 * it + 1, 1)

        @block.tensor
        def _(pe):
            m_ = nc.tensor

            def turn(i, par):
                wait(pe, lnr, i + 1)
                wait(pe, ocp, i - 1)
                for n in range(TT):
                    last = m_.transpose(H1[par][:, n * P:(n + 1) * P], xn[:, par, n, :], ident[:])
                last.then_inc(xt, 1)
                wait(pe, ocp, i + 1)
                wait(pe, tcp, i - 1)
                m_.matmul(H2[par], S["twist"][:], o[:, bass.ds(i, 1), :].rearrange("p a n -> p (a n)"),
                          start=True, stop=True).then_inc(tw, 1)
            over_chunks(pe, turn)

            m_.matmul(H3[0:D // 2, 0:NB], S["g1"][:], sums[:], start=True, stop=True).then_inc(gmm, 1)
            pe.wait_ge(gact, 1)
            m_.matmul(H3[0:D // 4, 0:NB], S["g2"][:], gh1[:], start=True, stop=True).then_inc(gmm, 1)
            pe.wait_ge(gact, 2)
            m_.matmul(H3[:, 0:NB], S["g3"][:], gh2[:], start=True, stop=True).then_inc(gmm, 1)
            pe.wait_ge(gact, 3)
            pe.wait_ge(tcp, NCH)

            def layer1(k, j):
                n = HB * k + j
                wait(pe, odone, HB * (k - 2) + j + 1 if k >= 2 else 0)
                wait(pe, g1a, n - 1)
                m_.matmul(H1[j % 2], S["w1"][:], o[:, HB * (k % 2) + j, :], start=True, stop=True).then_inc(h1m, 1)

            def layer2(k, j):
                n = HB * k + j
                pe.wait_ge(g1a, n + 1)
                if j % 2 == 0:
                    wait(pe, g2a, n // 2 - 1)
                r = 64 * (j % 2)
                m_.matmul(H2[j // 2][r:r + 64, :], S["w2"][:], h1[:, j % 2, :], start=True, stop=True).then_inc(h2m, 1)

            def layer3(k, n):
                pe.wait_ge(g2a, 2 * k + n + 1)
                wait(pe, g3a, k)
                m_.matmul(H3[64 * n:64 * n + 64, :], S["w3"][:], h2[:, n, :], start=True, stop=True).then_inc(h3m, 1)

            def layer4(k):
                pe.wait_ge(g3a, k + 1)
                wait(pe, tha, k)
                m_.matmul(H4, S["w4"][:], h3[:], start=True, stop=True).then_inc(h4m, 1)

            def spread(k, j):
                n = HB * k + j
                if j == 0:
                    pe.wait_ge(cr, k + 1)
                wait(pe, zr, n - 1)
                m_.matmul(BC[j % 2], S["pick"][:, j, :], chigh[:], start=True, stop=False)
                m_.matmul(BC[j % 2], S["pick"][:, j, :], clow[:], start=False, stop=True).then_inc(bcm, 1)

            for k in range(STEPS):
                layer1(k, 0)
                if k:
                    layer3(k - 1, 1)
                layer1(k, 1)
                if k:
                    layer4(k - 1)
                layer2(k, 0)
                layer1(k, 2)
                if k:
                    spread(k - 1, 0)
                layer2(k, 1)
                layer1(k, 3)
                if k:
                    spread(k - 1, 1)
                layer2(k, 2)
                if k:
                    spread(k - 1, 2)
                layer3(k, 0)
                layer2(k, 3)
                if k:
                    spread(k - 1, 3)
            k = STEPS - 1
            layer3(k, 1)
            layer4(k)
            pe.wait_ge(g1a, HB * STEPS)

            def turn_back(n):
                pe.wait_ge(odone, HB * (STEPS - 2) + n + 1)
                wait(pe, xdone, n - 1)
                for q in range(TT):
                    last = m_.transpose(H1[n % 2][:, q * P:(q + 1) * P], o[:, n, q * P:(q + 1) * P], ident[:])
                last.then_inc(fin, 1)
            for j in range(HB):
                turn_back(j)
                spread(k, j)
            for j in range(HB):
                turn_back(HB + j)

        @block.scalar
        def _(act):
            a = nc.scalar

            def copies(i, par):
                act.wait_ge(xt, i + 1)
                for n in range(2):
                    last = a.activation(o[:, bass.ds(i, 1), n * T:(n + 1) * T].rearrange("p a n -> p (a n)"),
                                        H1[par][:, n * T:(n + 1) * T], ACT.Identity,
                                        accum_out=sums[:, bass.ds(2 * i + n, 1)])
                last.then_inc(ocp, 1)
                act.wait_ge(tw, i + 1)
                a.activation(t[:, bass.ds(i, 1), :].rearrange("p a n -> p (a n)"), H2[par], ACT.Identity).then_inc(tcp, 1)
            over_chunks(act, copies)

            act.wait_ge(gmm, 1)
            a.activation(gh1[:], H3[0:D // 2, 0:NB], ACT.Gelu, bias=S["gb1"][:], scale=1.0 / T).then_inc(gact, 1)
            act.wait_ge(gmm, 2)
            a.activation(gh2[:], H3[0:D // 4, 0:NB], ACT.Gelu, bias=S["gb2"][:]).then_inc(gact, 1)
            act.wait_ge(gmm, 3)
            a.activation(gate[:], H3[:, 0:NB], ACT.Tanh, bias=S["gb3"][:], scale=0.5).then_inc(gact, 1)

            def gelu1(k, j):
                n = HB * k + j
                act.wait_ge(h1m, n + 1)
                wait(act, h2m, n - 1)
                a.activation(h1[:, j % 2, :], H1[j % 2], ACT.Gelu, bias=S["cb1"][:]).then_inc(g1a, 1)

            def gelu2(k, n):
                act.wait_ge(h2m, HB * k + 2 * n + 2)
                wait(act, h3m, 2 * k + n - 1)
                a.activation(h2[:, n, :], H2[n], ACT.Gelu, bias=S["cb2"][:]).then_inc(g2a, 1)

            def gelu3(k):
                act.wait_ge(h3m, 2 * k + 2)
                wait(act, h4m, k)
                a.activation(h3[:], H3, ACT.Gelu, bias=S["cb3"][:]).then_inc(g3a, 1)

            def tanh(k):
                act.wait_ge(h4m, k + 1)
                wait(act, cr, k)
                a.activation(th[:], H4, ACT.Tanh, bias=S["cb4"][:], scale=0.5).then_inc(tha, 1)

            for k in range(STEPS):
                gelu1(k, 0)
                if k:
                    gelu2(k - 1, 1)
                    gelu3(k - 1)
                gelu1(k, 1)
                if k:
                    tanh(k - 1)
                gelu1(k, 2)
                gelu1(k, 3)
                gelu2(k, 0)
            k = STEPS - 1
            gelu2(k, 1)
            gelu3(k)
            tanh(k)

        @block.vector
        def _(dve):
            v = nc.vector

            def source(i, n):
                return X[:, bass.ds(TT * i + n, 1), :].rearrange("p a d -> p (a d)")

            def norm_sums(i):
                for n in range(TT):
                    last = v.bn_stats(stats[:, n, :], source(i, n))
                last.then_inc(ln_step, 1)

            def norm_moments(i, par):
                for n in range(TT):
                    last = v.bn_aggr(mv[:, par, n, :], stats[:, n, :])
                last.then_inc(ln_step, 1)
                dve.wait_ge(ln_step, 2 * i + 2)
                v.tensor_scalar(veps[:, par, :], mv[:, par, :, 1], EPS, None, ALU.add).then_inc(vepsr, 1)

            def norm_apply(i, par):
                dve.wait_ge(rsq, i + 1)
                wait(dve, xt, i - 1)
                for n in range(TT):
                    last = v.tensor_scalar(xn[:, par, n, :], source(i, n), mv[:, par, n, 0:1], rstd[:, par, n:n + 1],
                                           ALU.subtract, ALU.mult)
                last.then_inc(lnr, 1)

            def norm(i, par):
                norm_sums(i)
                dve.wait_ge(ln_step, 2 * i + 1)
                if not (isinstance(i, int) and i == 0):
                    norm_apply(i - 1, 1 - par)
                norm_moments(i, par)
            over_chunks(dve, norm)
            norm_apply(NCH - 1, 1)

            dve.wait_ge(gact, 3)
            v.tensor_scalar(offs[:], gate[:], S["ar7"][:], 0.1, ALU.mult, ALU.add).then_inc(off_step, 1)
            dve.wait_ge(off_step, 1)
            for j in range(HB):
                r = slice(32 * j, 32 * j + 32)
                last = v.tensor_copy(off[r, :, :], offs[r, :].rearrange("p (a j h) -> p a j h", a=2, j=HB)[:, :, j, :])
            last.then_inc(goff, 1)
            dve.wait_ge(goff, 1)

            def coupling(k):
                dve.wait_ge(tha, k + 1)
                for n in range(2):
                    last = v.tensor_scalar(c[:, n * T:(n + 1) * T], th[:, n * T:(n + 1) * T], S["ar3"][:],
                                           off[:, k % 2, n:n + 1], ALU.mult, ALU.add)
                last.then_inc(c_step, 1)
                dve.wait_ge(c_step, 2 * k + 1)
                wait(dve, bcm, HB * k)
                v.tensor_copy(chigh[:], c[:]).then_inc(c_step, 1)
                dve.wait_ge(c_step, 2 * k + 2)
                v.tensor_tensor(clow[:], c[:], chigh[:].bitcast(F32), ALU.subtract).then_inc(cr, 1)

            def update(k, j):
                n, q = HB * k + j, HB * (k % 2) + j
                again = k < STEPS - 2
                dve.wait_ge(bcm, n + 1)
                wait(dve, tdone, HB * (k - 2) + j + 1 if k >= 2 else 0)
                z = v.tensor_tensor(z_t[:, j % 2, :], BC[j % 2], t[:, q, :], ALU.mult)
                if again:
                    wait(dve, tdone, n - 1)
                    z = v.tensor_tensor(z_o[:, j % 2, :], BC[j % 2], o[:, q, :], ALU.mult)
                z.then_inc(zr, 1)
                dve.wait_ge(zr, n + 1)
                v.tensor_tensor(o[:, q, :], o[:, q, :], z_t[:, j % 2, :], ALU.add).then_inc(odone, 1)

            dve.wait_ge(tcp, NCH)
            for k in range(1, STEPS):
                coupling(k - 1)
                for j in range(HB):
                    update(k - 1, j)

            def add(n):
                dve.wait_ge(fin, n + 1)
                x = X[:, TT * n:TT * (n + 1), :].rearrange("p a d -> p (a d)")
                v.tensor_tensor(x, H1[n % 2], x, ALU.add).then_inc(xdone, 1)
            k = STEPS - 1
            coupling(k)
            for j in range(HB):
                add(j)
                update(k, j)
            for j in range(HB):
                add(HB + j)

        @block.gpsimd
        def _(pool):
            def inverse_root(i, par):
                pool.wait_ge(vepsr, i + 1)
                nc.gpsimd.tensor_tensor(rstd[:, par, :], veps[:, par, :], S["minus_half"][:, 0:TT], ALU.pow).then_inc(rsq, 1)
            over_chunks(pool, inverse_root)
            for k in range(STEPS - 2):
                for j in range(HB):
                    q = HB * (k % 2) + j
                    pool.wait_ge(zr, HB * k + j + 1)
                    nc.gpsimd.tensor_tensor(t[:, q, :], t[:, q, :], z_o[:, j % 2, :], ALU.subtract).then_inc(tdone, 1)

        if out is not None:
            tiles = out.rearrange("b (t p) d -> p (b t) d", p=P)

            @block.sync
            def _(sp):
                for n in range(NCH):
                    sp.wait_ge(xdone, n + 1)
                    sp.dma_start(tiles[:, TT * n:TT * (n + 1), :], X[:, TT * n:TT * (n + 1), :]).then_inc(stored, 16)
                sp.wait_ge(stored, 16 * NCH)


INPUTS = ["L0_attn_a_x", "L0_attn_a_w_qkv", "L0_attn_a_w_out", "L0_attn_b_ln_gamma", "L0_attn_b_ln_beta",
          "L0_attn_b_W_qkv", "L0_attn_b_b_qkv", "L0_attn_b_W_proj", "L0_attn_b_b_proj",
          "L0_ffn_cn_w1", "L0_ffn_cn_b1", "L0_ffn_cn_w2", "L0_ffn_cn_b2", "L0_ffn_cn_w3", "L0_ffn_cn_b3",
          "L0_ffn_cn_w4", "L0_ffn_cn_b4", "L0_ffn_gc_w1", "L0_ffn_gc_b1", "L0_ffn_gc_w2", "L0_ffn_gc_b2",
          "L0_ffn_gc_w3", "L0_ffn_gc_b3", "L0_ffn_adaptive_range"]


def kernel(**inputs):
    import numpy as _np
    import concourse.bacc as _bacc
    from concourse import mybir as _mybir
    from concourse.bass_utils import run_bass_kernel_spmd as _run

    nc = _bacc.Bacc("TRN2", target_bir_lowering=False, num_devices=1)
    arrays, args = {}, []
    for name in INPUTS:
        a = _np.ascontiguousarray(inputs[name])
        arrays["in_" + name] = a
        args.append(nc.dram_tensor("in_" + name, a.shape, _mybir.dt.from_np(a.dtype), kind="ExternalInput").ap())
    out = nc.dram_tensor("out_x", (NB, T, D), _mybir.dt.float32, kind="ExternalOutput").ap()
    build(nc, *args, out)
    r = _run(nc, [arrays], core_ids=[0])
    return r.results[0]["out_x"]
```

```python
from contextlib import ExitStack

import numpy as np
import concourse.bass as bass
from concourse import mybir
from concourse.alu_op_type import AluOpType as ALU

ACT = mybir.ActivationFunctionType
F32 = mybir.dt.float32
F32R = mybir.dt.float32r
BF16 = mybir.dt.bfloat16
AX = mybir.AxisListType.X

NB, T, D = 16, 256, 128
P = 128
NT = NB * T // P
H, DH = 16, 8
G, HG = 4, 4
GW = HG * DH
SL = 3 * GW
VB = 48
EPS = 1e-5
NEG = -1e30
BIG = 3e38
CH = 512
NCH = NB * T // CH
CYCLES = 3
SIGNS = (1.0, -1.0, 1.0)


class Handed:
    pass


def wait(eng, sem, value):
    if isinstance(value, int) and value <= 0:
        return
    eng.wait_ge(sem, value)


def over_batches(eng, body):
    for b in (0, 1):
        body(b, b % 2, b, 2)
    with eng.Fori(1, NB // 2 - 1) as it:
        body(2 * it, 0, 2, 2)
        body(2 * it + 1, 1, 2, 2)
    for b in (NB - 2, NB - 1):
        body(b, b % 2, 2, NB - 1 - b)


def build(nc, x, w_qkv, w_out, ln_gamma, ln_beta, W_qkv, b_qkv, W_proj, b_proj,
          cn_w1, cn_b1, cn_w2, cn_b2, cn_w3, cn_b3, cn_w4, cn_b4,
          gc_w1, gc_b1, gc_w2, gc_b2, gc_w3, gc_b3, adaptive_range, out):
    with ExitStack() as ctx:
        def sb(name, shape, dt=F32):
            return ctx.enter_context(nc.sbuf_tensor(name, shape, dt))

        S = {}
        S["X"] = sb("X", [P, NT, D])
        S["N"] = sb("N", [P, NT, D])
        S["ident"] = sb("ident", [P, P])
        S["minus_half"] = sb("minus_half", [P, 4])
        S["ident_h"] = sb("ident_h", [P, P], BF16)
        S["causal_qk"] = sb("causal_qk", [P, 2, P], BF16)
        S["cap"] = sb("cap", [P, P])
        S["head_rows"] = sb("head_rows", [P, HG])
        S["max_row"] = sb("max_row", [P, HG])
        for ph in "ab":
            S["wqkh" + ph] = sb("wqkh" + ph, [P, 2, G, SL], F32R)
            S["wqkl" + ph] = sb("wqkl" + ph, [P, 2, G, SL], F32R)
            S["wv" + ph] = sb("wv" + ph, [P, D])
            S["wo" + ph] = sb("wo" + ph, [P, D])
        S["bqk"] = sb("bqk", [P, 2, G])
        S["bv"] = sb("bv", [P, D])
        S["bproj"] = sb("bproj", [P, D])
        S["gamma"] = sb("gamma", [P, 1])
        S["beta"] = sb("beta", [P, 1])
        S["w1"] = sb("w1", [P, D])
        S["w2"] = sb("w2", [P, D // 2])
        S["blocks"] = sb("blocks", [P, 4])
        S["w3"] = sb("w3", [P, D // 2])
        S["w4"] = sb("w4", [P, 4])
        S["w4c"] = sb("w4c", [P, 1])
        S["cb1"] = sb("cb1", [P, 1])
        S["cb2"] = sb("cb2", [P, 1])
        S["cb3"] = sb("cb3", [P, 1])
        S["cb4"] = sb("cb4", [P, 1])
        S["g1"] = sb("g1", [P, D // 2])
        S["g2"] = sb("g2", [D // 2, D // 4])
        S["g3"] = sb("g3", [D // 4, P])
        S["g3c"] = sb("g3c", [D // 4, 1])
        S["gb1"] = sb("gb1", [D // 2, 1])
        S["gb2"] = sb("gb2", [D // 4, 1])
        S["gb3"] = sb("gb3", [P, 1])
        S["ar"] = sb("ar", [P, 1])
        S["ar3"] = sb("ar3", [P, 3])
        S["ar7"] = sb("ar7", [P, 1])

        S["loaded"] = ctx.enter_context(nc.semaphore("loaded"))
        S["prepared"] = ctx.enter_context(nc.semaphore("prepared"))
        S["wb"] = sb("wb_in", [P, 3 * D])
        later = [
            (S["wb"][:], W_qkv), (S["gamma"][:], ln_gamma.unsqueeze(1)), (S["beta"][:], ln_beta.unsqueeze(1)),
            (S["bproj"][:], b_proj.partition_broadcast(P)),
            (S["w1"][:], cn_w1), (S["w2"][:], cn_w2), (S["g1"][:], gc_w1), (S["g2"][:], gc_w2),
            (S["cb1"][:], cn_b1.unsqueeze(1)), (S["gb1"][:], gc_b1.unsqueeze(1)), (S["gb2"][:], gc_b2.unsqueeze(1)),
            (S["g3c"][:], gc_w3), (S["cb4"][:], cn_b4.partition_broadcast(P)),
            (S["gb3"][:], gc_b3.partition_broadcast(P)), (S["ar"][:], adaptive_range.partition_broadcast(P)),
            (S["w3"][0:64, 0:32], cn_w3), (S["w3"][64:128, 32:64], cn_w3),
        ]
        for w in range(2):
            for n in range(2):
                c = 2 * D + 64 * n + 32 * w
                later.append((S["bv"][:, 64 * w + 32 * n:64 * w + 32 * n + 32], b_qkv[c:c + 32].partition_broadcast(P)))
        for n in range(2):
            later.append((S["cb2"][64 * n:64 * n + 64, :], cn_b2.unsqueeze(1)))
        for n in range(4):
            later.append((S["cb3"][32 * n:32 * n + 32, :], cn_b3.unsqueeze(1)))
            later.append((S["w4c"][32 * n:32 * n + 32, :], cn_w4))
        for n in range(3):
            later.append((S["bqk"][GW * n:GW * n + GW, :, :], b_qkv[0:2 * D].rearrange("(n g r) -> r n g", n=2, g=G)))
        for h in range(H):
            g, i = h // HG, h % HG
            r = 64 * (g // 2) + 16 * i + 8 * (g % 2)
            later.append((S["wob"][r:r + 8, :], W_proj[8 * h:8 * h + 8, :]))
        S["later"] = later
        ctx.enter_context(nc.allow_non_contiguous_dma(reason="a few hundred bias values, once"))

        S["km"] = sb("km", [P, G, HG, T], F32R)
        S["vx"] = sb("vx", [P, 2, 2, 2 * HG * VB])
        S["mw"] = sb("mw", [P, 2, 2, P - SL])
        for name, shape, dt in (
                ("stats", [P, 2, 6], F32), ("mv", [P, 2, 2], F32), ("veps", [P, 2], F32), ("rstd", [P, 2], F32),
                ("centred", [P, 2, D], F32), ("xn0", [P, 2, D], F32), ("xn", [P, 2, D], F32),
                ("xnT", [P, 2, T], F32),
                ("xh", [P, 2, T], F32R), ("xl", [P, 2, T], F32R),
                ("qk", [P, G, 2, T], F32R),
                ("rmax", [P, 2, HG, 3], F32),
                ("probs", [P, 2, HG, 512], F32),
                ("os", [P, 2 * T], F32), ("rec", [P, 4 * 2 * HG], F32), ("y", [P, 2, D], F32), ("yT", [P, T], F32),
                ("ostats", [P, 2, 6], F32),
                ("omv", [P, 2, 2, 2], F32),
                ("oveps", [P, 2, 2], F32), ("orstd", [P, 2, 2], F32), ("ocentred", [P, 2, 2, D], F32)):
            S[name] = sb(name, shape, dt)
        for name, shape in (
                ("O1", [P, NT, D]),
                ("oT", [P, 2, NCH // 2, CH]),
                ("prod", [P, 2, CH // P, D]),
                ("sums", [P, NB]),
                ("gh1", [D // 2, NB // 2]), ("gh2", [D // 4, NB // 2]),
                ("gate", [P, 2, NB // 2]),
                ("offs", [P, 2, NB // 2]),
                ("off", [P, 2, NCH // 2 * CH // P, 3]),
                ("h1", [P, 2, CH]), ("h2", [P, 2, CH]), ("h3", [P, CH]),
                ("th", [P, NCH // 2 * CH // P]), ("cm", [P, NCH // 2 * CH // P, 3]),
                ("c", [P, 2, NCH // 2 * CH // P, 3])):
            S[name] = sb(name, shape)

        setup(nc, S, x, w_qkv, w_out)
        S["ctx"] = ctx
        S["ps"] = ctx.enter_context(nc.psum_tensor("ps", [P, 8, 512], F32))
        block = ctx.enter_context(nc.Block())
        attention_a = attention(nc, S, "a", block, None)
        feed_forward_f = feed_forward(nc, S, "f", block, attention_a, None)
        attention_b = attention(nc, S, "b", block, feed_forward_f)
        feed_forward(nc, S, "s", block, attention_b, out)


def slots(v):
    return v.rearrange("p (g r) -> p g r", r=GW).unsqueeze(2).broadcast_to([v.shape[0], G, 3, GW])


def in_slots(w):
    return w.rearrange("p g (s r) -> p g s r", s=3)


def setup(nc, S, x, w_qkv, w_out):
    with ExitStack() as ctx:
        wa = ctx.enter_context(nc.sbuf_tensor("set_wa", [P, 3, D], F32))
        woa = ctx.enter_context(nc.sbuf_tensor("set_woa", [P, D], F32))
        woap = ctx.enter_context(nc.sbuf_tensor("woap", [P, D], F32))
        band = ctx.enter_context(nc.sbuf_tensor("band", [P, HG, 4], F32))
        mask = ctx.enter_context(nc.sbuf_tensor("mask", [P, P], F32))
        ps = ctx.enter_context(nc.psum_tensor("ps_setup", [P, 4, 512], F32))

        def sem(name):
            return ctx.enter_context(nc.semaphore("set_" + name))
        x_in, w_in = sem("x_in"), sem("w_in")
        zeroed, shaped, high = sem("zeroed"), sem("shaped"), sem("high")
        permuted, turned = sem("permuted"), sem("turned")
        block = ctx.enter_context(nc.Block())
        X = S["X"]
        tiles = x.rearrange("b (t p) d -> p (b t) d", p=P)

        @block.sync
        def _(sp):
            for n in range(4):
                sp.dma_start(X[:, 8 * n:8 * n + 8, :], tiles[:, 8 * n:8 * n + 8, :]).then_inc(x_in, 16)
            sp.wait_ge(x_in, 64)

        @block.gpsimd
        def _(pool):
            g = nc.gpsimd
            g.memset(S["ident"][:], 0.0)
            g.memset(mask[:], 0.0)
            g.memset(S["cap"][:], BIG)
            g.memset(band[:], 1.0)
            g.memset(S["max_row"][:], 0.0)
            g.memset(S["blocks"][:], 1.0)
            g.memset(S["mw"][:], 0.0)
            g.memset(S["vx"][:], 0.0)
            g.memset(S["minus_half"][:], -0.5).then_inc(zeroed, 1)
            pool.wait_ge(zeroed, 1)
            g.affine_select(out=S["ident"][:], in_=S["ident"][:], compare_op=ALU.not_equal, fill=1.0,
                            base=0, pattern=[[-1, P]], channel_multiplier=1).then_inc(shaped, 1)
            g.affine_select(out=mask[:], in_=mask[:], compare_op=ALU.is_ge, fill=NEG,
                            base=0, pattern=[[-1, P]], channel_multiplier=1)
            g.affine_select(out=S["cap"][:], in_=S["cap"][:], compare_op=ALU.is_ge, fill=0.0,
                            base=0, pattern=[[1, P]], channel_multiplier=-1)
            g.affine_select(out=S["max_row"][:], in_=S["max_row"][:], compare_op=ALU.not_equal, fill=1.0,
                            base=-SL, pattern=[[-DH, HG]], channel_multiplier=1)
            g.affine_select(out=band[:], in_=band[:], compare_op=ALU.is_ge, fill=0.0,
                            base=0, pattern=[[-DH, HG], [-GW, 4]], channel_multiplier=1)
            g.affine_select(out=S["blocks"][:], in_=S["blocks"][:], compare_op=ALU.is_ge, fill=0.0,
                            base=0, pattern=[[-GW, 4]], channel_multiplier=1).then_inc(shaped, 1)
            pool.wait_ge(shaped, 2)
            g.affine_select(out=band[:], in_=band[:], compare_op=ALU.is_ge, fill=0.0,
                            base=DH - 1, pattern=[[DH, HG], [GW, 4]], channel_multiplier=-1)
            g.affine_select(out=S["blocks"][:], in_=S["blocks"][:], compare_op=ALU.is_ge, fill=0.0,
                            base=GW - 1, pattern=[[GW, 4]], channel_multiplier=-1).then_inc(shaped, 1)
            g.memset(S["w3"][:], 0.0)
            for w in range(2):
                ones = S["vx"][:].rearrange("p a t (n e) -> p (a t n) e", e=VB)[:, :, 32 * w + DH:32 * w + DH + 1]
                g.memset(ones, 1.0)

        @block.scalar
        def _(act):
            act.dma_start(wa[:], w_qkv.rearrange("(t p) c -> p t c", p=P)).then_inc(w_in, 16)
            act.dma_start(woa[:], w_out).then_inc(w_in, 16)
            act.wait_ge(turned, 1)
            for n in range(2):
                last = nc.scalar.activation(in_slots(S["wqkha"][:, n]), slots(ps[:, n, 0:D]), ACT.Identity)
            last.then_inc(high, 1)

        @block.vector
        def _(dve):
            v = nc.vector
            dve.wait_ge(w_in, 32)
            for n in range(2):
                last = v.tensor_copy(woap[:, 64 * n:64 * n + 64].rearrange("p (i w d) -> p i w d", i=HG, w=2),
                                     woa[:, 64 * n:64 * n + 64].rearrange("p (w i d) -> p i w d", w=2, i=HG))
            last.then_inc(permuted, 1)
            dve.wait_ge(shaped, 3)
            for g in range(G):
                v.tensor_copy(S["km"][SL:P, g, :, :], S["max_row"][SL:P, :].unsqueeze(2).broadcast_to([P - SL, HG, T]))
            v.tensor_reduce(S["head_rows"][:], band[:], AX, ALU.add)
            v.tensor_copy(S["ident_h"][:], S["ident"][:])
            v.tensor_copy(S["causal_qk"][:], mask[:].unsqueeze(1).broadcast_to([P, 2, P]))
            dve.wait_ge(turned, 2)
            v.tensor_copy(S["wva"][:].rearrange("p (w n r) -> p w n r", w=2, n=2),
                          ps[:, 2, 0:D].rearrange("p (n w r) -> p w n r", n=2, w=2))
            v.tensor_copy(S["woa"][:], ps[:, 3, 0:D])
            dve.wait_ge(high, 1)
            for n in range(2):
                v.tensor_tensor(in_slots(S["wqkla"][:, n]), slots(ps[:, n, 0:D]), in_slots(S["wqkha"][:, n]).bitcast(F32),
                                ALU.subtract)

        @block.tensor
        def _(pe):
            pe.wait_ge(w_in, 32)
            pe.wait_ge(shaped, 1)
            for n in range(2):
                last = nc.tensor.transpose(ps[:, n, 0:D], wa[:, n, :], S["ident"][:])
            last.then_inc(turned, 1)
            nc.tensor.transpose(ps[:, 2, 0:D], wa[:, 2, :], S["ident"][:])
            pe.wait_ge(permuted, 1)
            nc.tensor.transpose(ps[:, 3, 0:D], woap[:], S["ident"][:]).then_inc(turned, 1)


def attention(nc, S, ph, block, before):
    causal = ph == "a"
    scale = float(np.float32(1) / np.sqrt(DH).astype(np.float32)) if causal else float(DH ** -0.5)
    PW = 384 if causal else 512
    X, ident = S["X"], S["ident"]
    wqkh, wqkl, wv, wo = (S[name + ph] for name in ("wqkh", "wqkl", "wv", "wo"))

    def sem(name):
        return S["ctx"].enter_context(nc.semaphore(name + "_" + ph))

    km, vx, mw, stats, mv, veps, rstd, centred, xn0, xn, xnT, xh, xl, qk, rmax, probs, os_, rec, y, yT = (S[n] for n in (
        "km", "vx", "mw", "stats", "mv", "veps", "rstd", "centred", "xn0", "xn", "xnT", "xh", "xl", "qk", "rmax",
        "probs", "os", "rec", "y", "yT"))
    ostats, omv, oveps, orstd, ocentred, ps = (S[n] for n in ("ostats", "omv", "oveps", "orstd", "ocentred", "ps"))
    MX = [ps[:, n, :] for n in range(2)]
    ST = [ps[:, 2 + n, :] for n in range(2)]
    TR, GEN, O, TAIL = (ps[:, n, :] for n in range(4, 8))

    xt, vg, gen, mt, mx, st, pv, ot, yt, pj = (sem(n) for n in (
        "xt_b", "vg_b", "gen_u", "mt_u", "mx_h", "st_h", "pv_u", "ot_b", "yt_b", "pj_b"))
    mrow, hi, kmr2, ex, osb, xnt, ytc = (sem(n) for n in (
        "mrow_u", "hi_u", "km2_u", "ex_h", "osb_b", "xnt_b", "ytc_b"))
    lo, red, mr, yn, res = (sem(n) for n in ("lo_u", "red_h", "mr_u", "yn_b", "res_b"))
    vxr = sem("vx_b")
    ln_step, max_step, rec_step = sem("ln_step"), sem("max_step"), sem("rec_step")
    vepsr, xlr = sem("veps_n"), sem("xl_b")
    xn0r, lnr = sem("xn0_b"), sem("ln_b")
    rsq, kmr = sem("rsqrt_n"), sem("km_u")
    out_step, ovepsr = sem("out_step"), sem("oveps_b")
    orsq, onr, biased = sem("orsqrt_b"), sem("out_norm_b"), sem("biased_b")
    NORMS = 1 if causal else 2
    MH = 2 if causal else 3
    REC_STEPS = 1 if causal else 2
    high_w = sem("high_w")
    kept, kept2 = sem("kept_u"), sem("kept2_u")

    def diagonal(scores):
        return scores.rearrange("p (n a k) -> p n a k", n=2, a=2)[:, :, 0, :]

    LOADED = 16 * len(S["later"])

    if causal:
        @block.sync
        def _(sp):
            for dst, src in S["later"]:
                sp.dma_start(dst, src).then_inc(S["loaded"], 16)
            sp.wait_ge(S["loaded"], LOADED)

    to_feed_forward = Handed()
    to_feed_forward.res, to_feed_forward.normed = res, onr

    def vx_columns(par, w):
        return vx[:, par, :, :].rearrange("p t (n e) -> p t n e", e=VB)[:, :, :, 32 * w:32 * w + DH]

    def v_columns(w):
        return TAIL[:, 0:T].rearrange("p (t w n d) -> p t w n d", t=2, w=2, d=DH)[:, :, w]

    @block.gpsimd
    def _(pool):
        def norm(b, k):
            n, final = NORMS * b + k, k == NORMS - 1
            pool.wait_ge(vepsr, n + 1)
            nc.gpsimd.tensor_tensor(rstd[:], veps[:], S["minus_half"][:, 0:2], ALU.pow)
            src = xn0[:] if k else X[:, bass.ds(2 * b, 2), :]
            mean = mv[:, :, 0].unsqueeze(2).broadcast_to([P, 2, D])
            nc.gpsimd.tensor_tensor(centred[:], src, mean, ALU.subtract).then_inc(rsq, 1)
            pool.wait_ge(rsq, n + 1)
            if final:
                wait(pool, xt, b)
            nc.gpsimd.tensor_tensor((xn if final else xn0)[:], centred[:], rstd[:].unsqueeze(2).broadcast_to([P, 2, D]),
                                    ALU.mult).then_inc(lnr if final else xn0r, 1)

        def mask_k(b, g):
            pool.wait_ge(lo, 4 * b + g + 1)
            nc.gpsimd.tensor_tensor(km[0:SL, g, 0:MH, :],
                                    qk[0:SL, g, 1, :].bitcast(F32).unsqueeze(1).broadcast_to([SL, MH, T]),
                                    S["head_rows"][0:SL, 0:MH].unsqueeze(2).broadcast_to([SL, MH, T]),
                                    ALU.mult).then_inc(kmr, 1)

        def keep_causal(b, g):
            for i in (0, 1):
                w = diagonal(probs[:, g % 2, i, :])
                last = nc.gpsimd.affine_select(out=w, in_=w, compare_op=ALU.is_ge, fill=0.0, base=0,
                                               pattern=[[0, 2], [1, P]], channel_multiplier=-1)
            last.then_inc(kept, 1)

        def add_bias(b):
            t = X[:, bass.ds(2 * b, 2), :]
            nc.gpsimd.tensor_tensor(t, t, S["bproj"][:].unsqueeze(1).broadcast_to([P, 2, D]), ALU.add).then_inc(biased, 1)

        def out_centre(b, par):
            pool.wait_ge(ovepsr, b + 1)
            nc.gpsimd.tensor_tensor(orstd[:, par, :], oveps[:, par, :], S["minus_half"][:, 0:2], ALU.pow)
            mean = omv[:, par, :, 0].unsqueeze(2).broadcast_to([P, 2, D])
            nc.gpsimd.tensor_tensor(ocentred[:, par], X[:, bass.ds(2 * b, 2), :], mean, ALU.subtract).then_inc(orsq, 1)

        def out_scale(b, par):
            nc.gpsimd.tensor_tensor(S["N"][:, bass.ds(2 * b, 2), :], ocentred[:, par],
                                    orstd[:, par, :].unsqueeze(2).broadcast_to([P, 2, D]), ALU.mult).then_inc(onr, 1)

        def batch(b, par, behind, ahead):
            for g in range(G):
                b3, g3 = b + (g + 3) // G, (g + 3) % G
                if behind == 2 and g == 2:
                    pool.wait_ge(orsq, b - 1)
                if causal:
                    pool.wait_ge(ex, 16 * b + 4 * g + 2)
                if ahead or g < 1:
                    mask_k(b3, g3)
                if causal:
                    keep_causal(b, g)
                if behind == 2 and g == 1:
                    out_centre(b - 2, par)
                if behind == 2 and g == 2:
                    out_scale(b - 2, par)
                if ahead == 2 and g >= G - 1 - NORMS and g < G - 1:
                    norm(b + 2, g - (G - 1 - NORMS))
                if ahead == 2 and g == 2 and not causal:
                    add_bias(b + 2)

        for b in (0, 1):
            for k in range(NORMS):
                norm(b, k)
        for g in range(3):
            mask_k(0, g)
        if not causal:
            add_bias(0)
            add_bias(1)
        over_batches(pool, batch)
        if causal:
            q = nc.gpsimd
            pool.wait_ge(S["loaded"], LOADED)
            q.tensor_scalar(S["w4"][:], S["blocks"][:], S["w4c"][:], None, ALU.mult)
            q.tensor_copy(S["g3"][:], S["g3c"][:].broadcast_to([D // 4, P]))
            for n, sign in enumerate(SIGNS):
                q.tensor_scalar(S["ar3"][:, n:n + 1], S["ar"][:], 0.3 * sign, None, ALU.mult)
            q.tensor_scalar(S["ar7"][:], S["ar"][:], 0.7, None, ALU.mult)
            q.tensor_scalar(S["cb4"][:], S["cb4"][:], 0.5, None, ALU.mult)
            q.tensor_scalar(S["gb3"][:], S["gb3"][:], 0.5, None, ALU.mult)
            q.tensor_copy(S["wvb"][:].rearrange("p (w n r) -> p w n r", w=2, n=2),
                          S["wb"][:, 2 * D:3 * D].rearrange("p (n w r) -> p w n r", n=2, w=2))
            pool.wait_ge(high_w, 1)
            for n in range(2):
                q.tensor_tensor(in_slots(S["wqklb"][:, n]), slots(S["wb"][:, n * D:(n + 1) * D]),
                                in_slots(S["wqkhb"][:, n]).bitcast(F32), ALU.subtract).then_inc(S["prepared"], 1)
        for b in (NB - 2, NB - 1):
            out_centre(b, b % 2)
            pool.wait_ge(orsq, b + 1)
            out_scale(b, b % 2)

    @block.tensor
    def _(pe):
        t_ = nc.tensor

        def turn_x(b):
            wait(pe, lnr, b + 1)
            wait(pe, res, b - 2)
            wait(pe, vxr, b)
            for t in range(2):
                last = t_.transpose(TAIL[:, t * P:(t + 1) * P], xn[:, t, :], ident[:])
            last.then_inc(xt, 1)

        def make_v(b, par):
            wait(pe, xnt, b + 1)
            wait(pe, ytc, b - 1)
            for t in range(2):
                last = t_.matmul(TAIL[:, t * P:(t + 1) * P], xnT[:, par, t * P:(t + 1) * P], wv[:], start=True, stop=True)
            last.then_inc(vg, 1)

        def make_qk(b, par, g, bank=GEN):
            u = 4 * b + g
            if g == 0:
                wait(pe, xlr, b + 1)
            if bank is GEN:
                wait(pe, lo, u)
            for n in range(2):
                part = bank[0:SL, n * T:(n + 1) * T]
                t_.matmul(part, wqkh[:, n, g, :], xl[:, par, :], start=True, stop=False)
                t_.matmul(part, wqkl[:, n, g, :], xh[:, par, :], start=False, stop=False)
                last = t_.matmul(part, wqkh[:, n, g, :], xh[:, par, :], start=False, stop=True)
            last.then_inc(gen, 1)

        def scores_for_max(b, g, heads):
            u = 4 * b + g
            for i in heads:
                h = 4 * u + i
                if i == 0:
                    wait(pe, kmr, u + 1)
                if i == MH:
                    wait(pe, kmr2, u + 1)
                wait(pe, red, h - 1)
                m, kh = MX[i % 2], km[0:SL, g, i, :]
                if causal:
                    t_.matmul(m[:, 0:P], qk[0:SL, g, 0, 0:P], kh[:, 0:P], start=True, stop=True)
                    t_.matmul(m[:, P:3 * P], qk[0:SL, g, 0, P:T], kh, start=False, stop=True, skip_group_check=True)
                    last = t_.matmul(diagonal(m), S["ident_h"][:], S["causal_qk"][:], start=False, stop=True,
                                     skip_group_check=True)
                else:
                    for t in range(2):
                        last = t_.matmul(m[:, t * T:(t + 1) * T], qk[0:SL, g, 0, t * P:(t + 1) * P], kh,
                                         start=True, stop=True)
                last.then_inc(mx, 1)

        def turn_max(b, g):
            u = 4 * b + g
            wait(pe, mr, u + 1)
            wait(pe, mrow, u)
            for t in range(2):
                last = t_.matmul(TR[SL:P, t * P:(t + 1) * P], mw[:, g % 2, t, :], ident[:], start=True, stop=True)
            last.then_inc(mt, 1)

        def scores(b, g, i):
            h = 16 * b + 4 * g + i
            if i == 0:
                wait(pe, mrow, 4 * b + g + 1)
            wait(pe, ex, h - 1)
            s, q = ST[i % 2], qk[:, g, 0, :]
            if causal:
                t_.matmul(s[:, T:3 * P], km[:, g, i, P:T], q[:, P:T], start=True, stop=True)
                last = t_.matmul(s[:, 0:T], km[:, g, i, 0:P], q, start=False, stop=True, skip_group_check=True)
            else:
                for c in range(2):
                    last = t_.matmul(s[:, c * T:(c + 1) * T], km[:, g, i, c * P:(c + 1) * P], q, start=True, stop=True)
            last.then_inc(st, 1)

        def times_v(b, par, g):
            if g == 0:
                wait(pe, osb, b)
                wait(pe, vxr, b + 1)
            if causal:
                wait(pe, kept, 4 * b + g + 1)
                wait(pe, kept2, 4 * b + g + 1)
            else:
                wait(pe, ex, 16 * b + 4 * g + 4)
            w, n = g % 2, g // 2
            for c in range(2):
                for i in range(HG):
                    skip = P if causal and c else 0
                    col = (n * HG + i) * VB + 16 * w
                    last = t_.matmul(O[32 * i:32 * i + 32, n * T + skip:(n + 1) * T], vx[:, par, c, col:col + 32],
                                     probs[:, g % 2, i, c * T:(c + 1) * T - skip], start=(g == 0 and c == 0),
                                     stop=(g == G - 1 and c == 1), skip_group_check=True)
            last.then_inc(pv, 1)

        def turn_o(b, has_x):
            wait(pe, osb, b + 1)
            wait(pe, res, b)
            if has_x:
                pe.wait_ge(xnt, b + 3)
            for t in range(2):
                for n in range(2):
                    last = t_.transpose(TAIL[:, (2 * t + n) * P:(2 * t + n + 1) * P],
                                        os_[:, n * T + t * P:n * T + (t + 1) * P], ident[:])
            last.then_inc(ot, 1)

        def turn_y(b):
            wait(pe, yn, b + 1)
            for t in range(2):
                last = t_.transpose(TAIL[:, t * P:(t + 1) * P], y[:, t, :], ident[:])
            last.then_inc(yt, 1)

        def project(b, has_v):
            wait(pe, ytc, b + 1)
            if has_v:
                pe.wait_ge(vxr, b + 3)
            for t in range(2):
                last = t_.matmul(TAIL[:, t * P:(t + 1) * P], yT[:, t * P:(t + 1) * P], wo[:], start=True, stop=True)
            last.then_inc(pj, 1)

        def batch(b, par, behind, ahead):
            more = ahead > 0
            for g in range(G):
                (b1, g1), (b2, g2), (b3, g3) = ((b + (g + n) // G, (g + n) % G) for n in (1, 2, 3))
                if more or g < 1:
                    make_qk(b3, (par + (g + 3) // G) % 2, g3)
                scores(b, g, 0)
                if more or g < 2:
                    scores_for_max(b2, g2, (0,))
                scores(b, g, 1)
                if more and g == 0:
                    turn_x(b + 1)
                if more or g < 2:
                    scores_for_max(b2, g2, (1,))
                if g and not causal:
                    times_v(b, par, g - 1)
                elif behind and not causal:
                    times_v(b - 1, 1 - par, G - 1)
                if more or g < 3:
                    turn_max(b1, g1)
                if g and causal:
                    times_v(b, par, g - 1)
                elif behind and causal:
                    times_v(b - 1, 1 - par, G - 1)
                if behind and g == 1:
                    turn_o(b - 1, more)
                if behind and g == 2:
                    turn_y(b - 1)
                if behind and g == 3:
                    project(b - 1, more)
                if more or g < 2:
                    scores_for_max(b2, g2, (2,))
                scores(b, g, 2)
                if more or g < 2:
                    scores_for_max(b2, g2, (3,))
                scores(b, g, 3)
                if more and g == 2:
                    make_v(b + 1, 1 - par)

        turn_x(0)
        make_qk(0, 0, 0)
        make_qk(0, 0, 1, ST[0])
        make_qk(0, 0, 2, ST[1])
        make_v(0, 0)
        scores_for_max(0, 0, range(HG))
        scores_for_max(0, 1, (0, 1))
        turn_max(0, 0)
        scores_for_max(0, 1, (2, 3))
        over_batches(pe, batch)
        to_feed_forward.times_v, to_feed_forward.turn_o = times_v, turn_o
        to_feed_forward.turn_y, to_feed_forward.project = turn_y, project

    @block.scalar
    def _(act):
        a = nc.scalar

        def copy_xT(b, par):
            act.wait_ge(xt, b + 1)
            for full in (xnT, xh):
                if causal:
                    last = a.activation(full[:, par, :], TAIL[:, 0:T], ACT.Identity)
                else:
                    last = a.activation(full[:, par, :], TAIL[:, 0:T], ACT.Identity, bias=S["beta"][:],
                                        scale=S["gamma"][:])
            last.then_inc(xnt, 1)

        def copy_v(b, par):
            act.wait_ge(vg, b + 1)
            for w in range(2):
                last = a.activation(vx_columns(par, w), v_columns(w), ACT.Identity)
            last.then_inc(vxr, 1)

        def high_parts(b, g, bank=GEN):
            act.wait_ge(gen, 4 * b + g + 1)
            if causal:
                a.activation(qk[0:SL, g, :, :].rearrange("p n t -> p (n t)"), bank[0:SL, :], ACT.Identity).then_inc(hi, 1)
            else:
                for n in range(2):
                    last = a.activation(qk[0:SL, g, n, :], bank[0:SL, n * T:(n + 1) * T], ACT.Identity,
                                        bias=S["bqk"][0:SL, n, g:g + 1])
                last.then_inc(hi, 1)

        def mask_k(b, g):
            act.wait_ge(lo, 4 * b + g + 1)
            for i in range(MH, HG):
                last = a.activation(km[0:SL, g, i, :], qk[0:SL, g, 1, :].bitcast(F32), ACT.Copy,
                                    scale=S["head_rows"][0:SL, i:i + 1])
            last.then_inc(kmr2, 1)

        def max_row(b, g):
            act.wait_ge(mt, 4 * b + g + 1)
            a.activation(qk[SL:P, g, 0, :], TR[SL:P, 0:T], ACT.Identity).then_inc(mrow, 1)

        def exponentials(b, g, i):
            act.wait_ge(st, 16 * b + 4 * g + i + 1)
            a.activation(probs[:, g % 2, i, 0:PW], ST[i % 2][:, 0:PW], ACT.Exp, scale=scale).then_inc(ex, 1)

        def copy_o(b):
            act.wait_ge(pv, 4 * b + 4)
            wait(act, ot, b)
            a.activation(os_[:], O, ACT.Identity).then_inc(osb, 1)

        def copy_yT(b):
            act.wait_ge(yt, b + 1)
            wait(act, pj, b)
            a.activation(yT[:], TAIL[:, 0:T], ACT.Identity).then_inc(ytc, 1)

        def batch(b, par, behind, ahead):
            more = ahead > 0
            for g in range(G):
                (b1, g1), (b3, g3) = ((b + (g + n) // G, (g + n) % G) for n in (1, 3))
                if causal and more and g == 3:
                    copy_v(b + 1, 1 - par)
                if more or g < 1:
                    high_parts(b3, g3)
                exponentials(b, g, 0)
                exponentials(b, g, 1)
                if more and g == 0:
                    copy_xT(b + 1, 1 - par)
                if behind and g == 0:
                    copy_o(b - 1)
                if more or g < 3:
                    max_row(b1, g1)
                if behind and g == 2:
                    copy_yT(b - 1)
                exponentials(b, g, 2)
                exponentials(b, g, 3)
                if more or g < 1:
                    mask_k(b3, g3)

        copy_xT(0, 0)
        high_parts(0, 0)
        high_parts(0, 1, ST[0])
        mask_k(0, 0)
        high_parts(0, 2, ST[1])
        mask_k(0, 1)
        mask_k(0, 2)
        if causal:
            copy_v(0, 0)
        max_row(0, 0)
        over_batches(act, batch)
        to_feed_forward.copy_o, to_feed_forward.copy_yT = copy_o, copy_yT
        if causal:
            act.wait_ge(S["loaded"], LOADED)
            for n in range(2):
                last = a.activation(in_slots(S["wqkhb"][:, n]), slots(S["wb"][:, n * D:(n + 1) * D]), ACT.Identity)
            last.then_inc(high_w, 1)

    @block.vector
    def _(dve):
        v = nc.vector

        def source(b, k, t):
            return xn0[:, t, :] if k else X[:, bass.ds(2 * b + t, 1), :].rearrange("p a d -> p (a d)")

        def norm_sums(b, k):
            if k:
                dve.wait_ge(xn0r, b + 1)
            else:
                wait(dve, lnr, b)
            for t in range(2):
                last = v.bn_stats(stats[:, t, :], source(b, k, t))
            last.then_inc(ln_step, 1)

        def norm_moments(b, k):
            for t in range(2):
                last = v.bn_aggr(mv[:, t, :], stats[:, t, :])
            last.then_inc(ln_step, 1)
            dve.wait_ge(ln_step, 2 * (NORMS * b + k) + 2)
            v.tensor_scalar(veps[:], mv[:, :, 1], EPS, None, ALU.add).then_inc(vepsr, 1)

        def copy_v(b, par):
            dve.wait_ge(vg, b + 1)
            for w in range(2):
                bv = S["bv"][:, 64 * w:64 * w + 64].rearrange("p (n d) -> p n d", d=DH)
                last = v.tensor_tensor(vx_columns(par, w), v_columns(w), bv.unsqueeze(1).broadcast_to([P, 2, 2 * HG, DH]),
                                       ALU.add)
            last.then_inc(vxr, 1)

        def low_x(b, par):
            dve.wait_ge(xnt, b + 1)
            v.tensor_tensor(xl[:, par, :], xnT[:, par, :], xh[:, par, :].bitcast(F32), ALU.subtract).then_inc(xlr, 1)

        def low_parts(b, g, bank=GEN):
            u = 4 * b + g
            dve.wait_ge(hi, u + 1)
            for n, r in ((0, 2 * GW), (1, GW)):
                part, full = qk[r:r + GW, g, n, :], bank[r:r + GW, n * T:(n + 1) * T]
                if causal:
                    last = v.tensor_tensor(part, full, part.bitcast(F32), ALU.subtract)
                else:
                    last = v.scalar_tensor_tensor(part, full, S["bqk"][r:r + GW, n, g:g + 1], part.bitcast(F32),
                                                  ALU.add, ALU.subtract)
            last.then_inc(lo, 1)

        def maxima(b, g, heads):
            for i in heads:
                h = 16 * b + 4 * g + i
                dve.wait_ge(mx, h + 1)
                if causal:
                    v.reduce_max(rmax[:, g % 2, i, 0:3], MX[i % 2][:, 0:3 * P].rearrange("p (n k) -> p n k", k=P), AX).then_inc(red, 1)
                else:
                    v.reduce_max(rmax[:, g % 2, i, 0:2], MX[i % 2].rearrange("p (n k) -> p n k", k=T), AX).then_inc(red, 1)

        def keep_causal(b, g):
            dve.wait_ge(ex, 16 * b + 4 * g + 4)
            w = probs[:, g % 2, 2:4, :].rearrange("p i (n a k) -> p i n a k", n=2, a=2)[:, :, :, 0, :]
            cap = S["cap"][:].unsqueeze(1).unsqueeze(1).broadcast_to([P, 2, 2, P])
            v.tensor_tensor(w, w, cap, ALU.min).then_inc(kept2, 1)

        def join_maxima(b, g):
            u, r = 4 * b + g, rmax[:, g % 2]
            dve.wait_ge(red, 4 * u + 4)
            v.tensor_tensor(r[:, :, 1], r[:, :, 1], r[:, :, 2], ALU.max).then_inc(max_step, 1)

        def spread_maxima(b, g):
            u, r = 4 * b + g, rmax[:, g % 2]
            if causal:
                dve.wait_ge(max_step, u + 1)
            else:
                dve.wait_ge(red, 4 * u + 4)
            wait(dve, mt, u - 1)
            o = mw[:, g % 2, :, :].rearrange("p t (i e) -> p t i e", e=DH)[:, :, :, 0]
            v.tensor_scalar(o, r[:, :, 0:2].rearrange("p i t -> p t i"), -1.0, None, ALU.mult).then_inc(mr, 1)

        def normalise(b):
            dve.wait_ge(ot, b + 1)
            n = REC_STEPS * b
            o = TAIL.rearrange("p (n e) -> p n e", e=2 * DH)
            if causal:
                v.reciprocal(rec[:], o[:, :, DH]).then_inc(rec_step, 1)
                dve.wait_ge(rec_step, n + 1)
            else:
                v.tensor_scalar(rec[:], o[:, :, DH], 1e-12, None, ALU.max).then_inc(rec_step, 1)
                dve.wait_ge(rec_step, n + 1)
                v.reciprocal(rec[:], rec[:]).then_inc(rec_step, 1)
                dve.wait_ge(rec_step, n + 2)
            wait(dve, yt, b)
            v.tensor_tensor(y[:].rearrange("p t (n d) -> p (t n) d", d=DH), o[:, :, 0:DH],
                            rec[:].unsqueeze(2).broadcast_to([P, 4 * 2 * HG, DH]), ALU.mult).then_inc(yn, 1)

        def add_residual(b):
            dve.wait_ge(pj, b + 1)
            if not causal:
                dve.wait_ge(biased, b + 1)
            t = X[:, bass.ds(2 * b, 2), :]
            v.tensor_tensor(t, TAIL[:, 0:T].rearrange("p (t d) -> p t d", t=2), t, ALU.add).then_inc(res, 1)

        def out_sums(b):
            for t in range(2):
                last = v.bn_stats(ostats[:, t, :], X[:, bass.ds(2 * b + t, 1), :].rearrange("p a d -> p (a d)"))
            last.then_inc(out_step, 1)

        def out_moments(b, par):
            for t in range(2):
                last = v.bn_aggr(omv[:, par, t, :], ostats[:, t, :])
            last.then_inc(out_step, 1)
            dve.wait_ge(out_step, 2 * b + 2)
            v.tensor_scalar(oveps[:, par, :], omv[:, par, :, 1], EPS, None, ALU.add).then_inc(ovepsr, 1)

        def batch(b, par, behind, ahead):
            more = ahead > 0
            for g in range(G):
                (b1, g1), (b2, g2), (b3, g3) = ((b + (g + n) // G, (g + n) % G) for n in (1, 2, 3))
                if causal and g:
                    keep_causal(b, g - 1)
                elif causal and behind:
                    keep_causal(b - 1, G - 1)
                if more and g == 3 and not causal:
                    copy_v(b + 1, 1 - par)
                if more or g < 2:
                    maxima(b2, g2, (0,))
                if not causal and (more or g < 3):
                    spread_maxima(b1, g1)
                if behind == 2 and g == 0:
                    dve.wait_ge(res, b - 1)
                if more or g < 2:
                    maxima(b2, g2, (1,))
                if more or g < 1:
                    low_parts(b3, g3)
                if more and g == 0:
                    low_x(b + 1, 1 - par)
                if behind and g == 1:
                    normalise(b - 1)
                norm = g - (G - 1 - NORMS)
                if ahead < 2 or norm < 0 or norm >= NORMS:
                    norm = None
                if behind == 2 and g == 0:
                    out_sums(b - 2)
                if norm is not None:
                    norm_sums(b + 2, norm)
                if more or g < 2:
                    maxima(b2, g2, (2,))
                if behind == 2 and g == 0:
                    dve.wait_ge(out_step, 2 * b - 3)
                if norm is not None:
                    dve.wait_ge(ln_step, 2 * (NORMS * (b + 2) + norm) + 1)
                if more or g < 2:
                    maxima(b2, g2, (3,))
                if behind == 2 and g == 0:
                    out_moments(b - 2, par)
                if norm is not None:
                    norm_moments(b + 2, norm)
                if causal and (more or g < 2):
                    join_maxima(b2, g2)
                    spread_maxima(b2, g2)
                if behind and g == 3:
                    add_residual(b - 1)

        def sums_and_moments(b, k):
            norm_sums(b, k)
            dve.wait_ge(ln_step, 2 * (NORMS * b + k) + 1)
            norm_moments(b, k)

        def feed_forward_part(n):
            if before:
                before.update_part(before.steps - 2 + n // 5, n % 5)

        for n in range(3):
            feed_forward_part(n)
        if before:
            dve.wait_ge(before.updated, before.chunks * (before.steps - 2) + 1)
        sums_and_moments(0, 0)
        feed_forward_part(3)
        feed_forward_part(4)
        if not causal:
            sums_and_moments(0, 1)
        feed_forward_part(5)
        sums_and_moments(1, 0)
        low_x(0, 0)
        feed_forward_part(6)
        if not causal:
            sums_and_moments(1, 1)
        low_parts(0, 0, GEN)
        feed_forward_part(7)
        low_parts(0, 1, ST[0])
        low_parts(0, 2, ST[1])
        feed_forward_part(8)
        if not causal:
            copy_v(0, 0)
        maxima(0, 0, range(HG))
        if causal:
            join_maxima(0, 0)
        spread_maxima(0, 0)
        feed_forward_part(9)
        maxima(0, 1, range(HG))
        if causal:
            join_maxima(0, 1)
            spread_maxima(0, 1)
        if before:
            dve.wait_ge(before.updated, before.chunks * before.steps)
        over_batches(dve, batch)
        if causal:
            keep_causal(NB - 1, G - 1)
        dve.wait_ge(res, NB - 1)
        out_sums(NB - 2)
        normalise(NB - 1)
        dve.wait_ge(out_step, 2 * NB - 3)
        dve.wait_ge(onr, NB - 3)
        out_moments(NB - 2, 0)
        add_residual(NB - 1)
        dve.wait_ge(res, NB)
        out_sums(NB - 1)
        dve.wait_ge(out_step, 2 * NB - 1)
        dve.wait_ge(onr, NB - 2)
        out_moments(NB - 1, 1)
    return to_feed_forward


def feed_forward(nc, S, ph, block, att, out):
    X, N, ident = S["X"], S["N"], S["ident"]
    TT = CH // P
    HB = NCH // 2
    STEPS = 2 * CYCLES

    def sem(name):
        return S["ctx"].enter_context(nc.semaphore(name + "_" + ph))

    O1, oT, prod, sums, gh1, gh2, gate, offs, off, h1, h2, h3, th, cm, c, ps = (S[n] for n in (
        "O1", "oT", "prod", "sums", "gh1", "gh2", "gate", "offs", "off", "h1", "h2", "h3", "th", "cm", "c", "ps"))
    before, after = (N, O1, N), (O1, N, X)
    H1, H2, TU = [ps[:, n, :] for n in (0, 1)], [ps[:, n, :] for n in (2, 3)], [ps[:, n, :] for n in (4, 5)]
    H3 = ps[:, 6, :]
    H4 = [ps[:, 7, :]] * (STEPS - 1) + [TU[0]]
    LOADED = 16 * len(S["later"])

    turned, gmm, h1m, h2m, h3m, h4m = (sem(n) for n in ("turned", "gate_mm", "h1m", "h2m", "h3m", "h4m"))
    copied, gact, g1a, g2a, g3a, tha = (sem(n) for n in ("copied", "gate_act", "g1a", "g2a", "g3a", "tha"))
    goff, off_step, c_step, cr = (sem(n) for n in ("offsets", "off_step", "c_step", "c_ready"))
    prod_step, updated = sem("prod_step"), sem("updated")
    to_attention = Handed()
    to_attention.updated, to_attention.steps, to_attention.chunks = updated, STEPS, HB
    based, stored = sem("based"), sem("stored")

    def tiles_of(buffer, k, j):
        n = TT * (HB * (k % 2) + j)
        return buffer[:, n:n + TT, :]

    @block.tensor
    def _(pe):
        m_ = nc.tensor

        def turn(k, j):
            n = HB * k + j
            wait(pe, updated, HB * (k - 2) + j + 1 if k >= 2 else 0)
            wait(pe, copied, n - 1)
            if k < 2:
                pe.wait_ge(att.normed, 2 * n + 2)
            src = tiles_of(before[k // 2], k, j)
            for q in range(TT):
                last = m_.transpose(TU[n % 2][:, q * P:(q + 1) * P], src[:, q, :], ident[:])
            last.then_inc(turned, 1)

        def gate_layer(blk, layer):
            cols = NB // 2
            if layer == 0:
                pe.wait_ge(copied, HB * (blk + 1))
                wait(pe, tha, blk)
                if blk == 0:
                    pe.wait_ge(att.res, NB)
                m_.matmul(H4[blk][0:D // 2, 0:cols], S["g1"][:], sums[:, cols * blk:cols * (blk + 1)], start=True,
                          stop=True).then_inc(gmm, 1)
            elif layer == 1:
                pe.wait_ge(gact, 3 * blk + 1)
                m_.matmul(H4[blk][0:D // 4, 0:cols], S["g2"][:], gh1[:], start=True, stop=True).then_inc(gmm, 1)
            else:
                pe.wait_ge(gact, 3 * blk + 2)
                m_.matmul(H4[blk][:, 0:cols], S["g3"][:], gh2[:], start=True, stop=True).then_inc(gmm, 1)

        def layer1(k, j):
            n = HB * k + j
            pe.wait_ge(copied, n + 1)
            wait(pe, g1a, n - 1)
            m_.matmul(H1[j % 2], S["w1"][:], oT[:, k % 2, j, :], start=True, stop=True).then_inc(h1m, 1)

        def layer2(k, j):
            n = HB * k + j
            pe.wait_ge(g1a, n + 1)
            if j % 2 == 0:
                wait(pe, g2a, n // 2 - 1)
            r = 64 * (j % 2)
            m_.matmul(H2[j // 2][r:r + 64, :], S["w2"][:], h1[:, j % 2, :], start=True, stop=True).then_inc(h2m, 1)

        def layer3(k, n):
            pe.wait_ge(g2a, 2 * k + n + 1)
            wait(pe, g3a, k)
            m_.matmul(H3[64 * n:64 * n + 64, :], S["w3"][:], h2[:, n, :], start=True, stop=True).then_inc(h3m, 1)

        def layer4(k):
            pe.wait_ge(g3a, k + 1)
            wait(pe, tha, k)
            if k < 2:
                pe.wait_ge(gact, 3 * (k + 1))
            for q in range(TT):
                last = m_.matmul(H4[k][:, HB * q:HB * (q + 1)], h3[:, q * P:(q + 1) * P], S["w4"][:], start=True, stop=True)
            last.then_inc(h4m, 1)

        pe.wait_ge(S["loaded"], LOADED)
        turn(0, 0)
        turn(0, 1)
        att.times_v(NB - 1, 1, G - 1)
        for k in range(STEPS):
            layer1(k, 0)
            turn(k, 2)
            if k == 0:
                att.turn_o(NB - 1, False)
            else:
                layer3(k - 1, 1)
            layer1(k, 1)
            turn(k, 3)
            layer2(k, 0)
            if k == 0:
                att.turn_y(NB - 1)
            else:
                layer4(k - 1)
            layer1(k, 2)
            layer2(k, 1)
            if k == 0:
                att.project(NB - 1, False)
            layer1(k, 3)
            layer2(k, 2)
            layer3(k, 0)
            if k == 0:
                pe.wait_ge(S["prepared"], 2)
            if k < 2:
                gate_layer(k, 0)
            if k < STEPS - 1:
                turn(k + 1, 0)
            if k < 2:
                gate_layer(k, 1)
            layer2(k, 3)
            if k < STEPS - 1:
                turn(k + 1, 1)
            if k < 2:
                gate_layer(k, 2)
        layer3(STEPS - 1, 1)
        layer4(STEPS - 1)

    @block.scalar
    def _(act):
        a = nc.scalar

        def copy(k, j):
            n = HB * k + j
            act.wait_ge(turned, n + 1)
            wait(act, h1m, HB * (k - 2) + j + 1 if k >= 2 else 0)
            if k < 2:
                for m in range(2):
                    last = a.activation(oT[:, k % 2, j, m * T:(m + 1) * T], TU[n % 2][:, m * T:(m + 1) * T],
                                        ACT.Identity, accum_out=sums[:, 2 * n + m:2 * n + m + 1])
            else:
                last = a.activation(oT[:, k % 2, j, :], TU[n % 2], ACT.Identity)
            last.then_inc(copied, 1)

        def gate_activation(blk, layer):
            cols = NB // 2
            act.wait_ge(gmm, 3 * blk + layer + 1)
            if layer == 0:
                a.activation(gh1[:], H4[blk][0:D // 2, 0:cols], ACT.Gelu, bias=S["gb1"][:], scale=1.0 / T).then_inc(gact, 1)
            elif layer == 1:
                a.activation(gh2[:], H4[blk][0:D // 4, 0:cols], ACT.Gelu, bias=S["gb2"][:]).then_inc(gact, 1)
            else:
                a.activation(gate[:, blk, :], H4[blk][:, 0:cols], ACT.Tanh, bias=S["gb3"][:], scale=0.5).then_inc(gact, 1)

        def gelu1(k, j):
            n = HB * k + j
            act.wait_ge(h1m, n + 1)
            wait(act, h2m, n - 1)
            a.activation(h1[:, j % 2, :], H1[j % 2], ACT.Gelu, bias=S["cb1"][:]).then_inc(g1a, 1)

        def gelu2(k, n):
            act.wait_ge(h2m, HB * k + 2 * n + 2)
            wait(act, h3m, 2 * k + n - 1)
            a.activation(h2[:, n, :], H2[n], ACT.Gelu, bias=S["cb2"][:]).then_inc(g2a, 1)

        def gelu3(k):
            act.wait_ge(h3m, 2 * k + 2)
            wait(act, h4m, k)
            a.activation(h3[:], H3, ACT.Gelu, bias=S["cb3"][:]).then_inc(g3a, 1)

        def tanh(k):
            act.wait_ge(h4m, k + 1)
            wait(act, c_step, k)
            a.activation(th[:], H4[k][:, 0:TT * HB], ACT.Tanh, bias=S["cb4"][:], scale=0.5).then_inc(tha, 1)

        act.wait_ge(S["loaded"], LOADED)
        copy(0, 0)
        copy(0, 1)
        att.copy_o(NB - 1)
        for k in range(STEPS):
            gelu1(k, 0)
            copy(k, 2)
            if k:
                gelu3(k - 1)
            gelu1(k, 1)
            copy(k, 3)
            if k == 0:
                att.copy_yT(NB - 1)
            else:
                tanh(k - 1)
            gelu1(k, 2)
            gelu2(k, 0)
            gelu1(k, 3)
            if k == 0:
                act.wait_ge(S["prepared"], 2)
            if k < 2:
                gate_activation(k, 0)
            if k < STEPS - 1:
                copy(k + 1, 0)
            if k < 2:
                gate_activation(k, 1)
            gelu2(k, 1)
            if k < STEPS - 1:
                copy(k + 1, 1)
            if k < 2:
                gate_activation(k, 2)
        gelu3(STEPS - 1)
        tanh(STEPS - 1)

    @block.vector
    def _(dve):
        v = nc.vector

        def offsets(blk):
            dve.wait_ge(gact, 3 * (blk + 1))
            v.tensor_scalar(offs[:, blk, :], gate[:, blk, :], S["ar7"][:], 0.1, ALU.mult, ALU.add).then_inc(off_step, 1)
            dve.wait_ge(off_step, blk + 1)
            batch_of = offs[:, blk, :].rearrange("p (j h) -> p h j", h=2).unsqueeze(2).broadcast_to([P, 2, TT // 2, HB])
            for n, sign in enumerate(SIGNS):
                last = v.tensor_scalar(off[:, blk, :, n].rearrange("p (h l j) -> p h l j", h=2, j=HB), batch_of,
                                       sign, None, ALU.mult)
            last.then_inc(goff, 1)

        def coupling(k):
            dve.wait_ge(tha, k + 1)
            v.tensor_tensor(cm[:], th[:].unsqueeze(2).broadcast_to([P, TT * HB, 3]),
                            S["ar3"][:].unsqueeze(1).broadcast_to([P, TT * HB, 3]), ALU.mult).then_inc(c_step, 1)
            dve.wait_ge(c_step, k + 1)
            if k < 2:
                dve.wait_ge(goff, k + 1)
            v.tensor_tensor(c[:, k % 2], cm[:], off[:, k % 2], ALU.add).then_inc(cr, 1)

        def update(k, j):
            n = HB * k + j
            src = tiles_of(before[k // 2], k, j)
            cj = c[:, k % 2].rearrange("p (q j) s -> p q j s", j=HB)[:, :, j, :]
            if j == 0:
                dve.wait_ge(cr, k + 1)
            for half in range(2):
                this, other = slice(64 * half, 64 * half + 64), slice(64 - 64 * half, 128 - 64 * half)
                last = v.tensor_tensor(prod[:, j % 2, :, this].rearrange("p q (s r) -> p q s r", s=2),
                                       src[:, :, other].rearrange("p q (s r) -> p q s r", s=2),
                                       cj[:, :, half:half + 2].unsqueeze(3).broadcast_to([P, TT, 2, D // 4]), ALU.mult)
            last.then_inc(prod_step, 1)

        def finish(k, j):
            n = HB * k + j
            dst = tiles_of(after[k // 2], k, j)
            dve.wait_ge(prod_step, n + 1)
            if k // 2 == CYCLES - 1:
                dve.wait_ge(based, n - HB * (STEPS - 2) + 1)
                base = dst
            else:
                base = tiles_of(before[k // 2], k, j)
            v.tensor_tensor(dst, base, prod[:, j % 2], ALU.add).then_inc(updated, 1)

        dve.wait_ge(S["prepared"], 2)

        def update_part(k, part):
            if part == 0:
                if k < 2:
                    offsets(k)
                coupling(k)
                update(k, 0)
            elif part < HB:
                if HB * k + part >= 2:
                    dve.wait_ge(updated, HB * k + part - 1)
                update(k, part)
                finish(k, part - 1)
            else:
                finish(k, HB - 1)

        for k in range(STEPS if out is not None else STEPS - 2):
            for part in range(HB + 1):
                update_part(k, part)
        to_attention.update_part = update_part

    @block.gpsimd
    def _(pool):
        for k in (STEPS - 2, STEPS - 1):
            for j in range(HB):
                pool.wait_ge(updated, HB * (k - 2) + j + 1)
                x = tiles_of(X, k, j)
                nc.gpsimd.tensor_tensor(x, x, tiles_of(before[CYCLES - 1], k, j), ALU.add).then_inc(based, 1)

    if out is not None:
        tiles = out.rearrange("b (t p) d -> p (b t) d", p=P)

        @block.sync
        def _(sp):
            for k in (STEPS - 2, STEPS - 1):
                for j in range(HB):
                    sp.wait_ge(updated, HB * k + j + 1)
                    sp.dma_start(tiles_of(tiles, k, j), tiles_of(X, k, j)).then_inc(stored, 16)
            sp.wait_ge(stored, 16 * NCH)
    return to_attention


INPUTS = ["L0_attn_a_x", "L0_attn_a_w_qkv", "L0_attn_a_w_out", "L0_attn_b_ln_gamma", "L0_attn_b_ln_beta",
          "L0_attn_b_W_qkv", "L0_attn_b_b_qkv", "L0_attn_b_W_proj", "L0_attn_b_b_proj",
          "L0_ffn_cn_w1", "L0_ffn_cn_b1", "L0_ffn_cn_w2", "L0_ffn_cn_b2", "L0_ffn_cn_w3", "L0_ffn_cn_b3",
          "L0_ffn_cn_w4", "L0_ffn_cn_b4", "L0_ffn_gc_w1", "L0_ffn_gc_b1", "L0_ffn_gc_w2", "L0_ffn_gc_b2",
          "L0_ffn_gc_w3", "L0_ffn_gc_b3", "L0_ffn_adaptive_range"]


def kernel(**inputs):
    import numpy as _np
    import concourse.bacc as _bacc
    from concourse import mybir as _mybir
    from concourse.bass_utils import run_bass_kernel_spmd as _run

    nc = _bacc.Bacc("TRN2", target_bir_lowering=False, num_devices=1)
    arrays, args = {}, []
    for name in INPUTS:
        a = _np.ascontiguousarray(inputs[name])
        arrays["in_" + name] = a
        args.append(nc.dram_tensor("in_" + name, a.shape, _mybir.dt.from_np(a.dtype), kind="ExternalInput").ap())
    out = nc.dram_tensor("out_x", (NB, T, D), _mybir.dt.float32, kind="ExternalOutput").ap()
    build(nc, *args, out)
    r = _run(nc, [arrays], core_ids=[0])
    return r.results[0]["out_x"]
```
